# Optimizing a Trainium2 kernel written in Bass

```python
import numpy as np
import jax
import jax.numpy as jnp

def _softmax(x, axis=-1):
    return jax.nn.softmax(x, axis=axis)

def _gelu(x):
    return jax.nn.gelu(x, approximate=True)

def _silu(x):
    return jax.nn.silu(x)

def _sigmoid(x):
    return jax.nn.sigmoid(x)

def _layernorm(x, axis=-1, eps=1e-05):
    m = jnp.mean(x, axis=axis, keepdims=True)
    v = jnp.var(x, axis=axis, keepdims=True)
    return (x - m) / jnp.sqrt(v + eps)

def _scatter_add(tgt, idx, src, axis=0):
    return tgt.at[idx].add(src)

def _segment_sum(src, seg, n):
    return jax.ops.segment_sum(src, seg, n)
kernel_name = 'mk_flamingo_gated_d1_seqx_r8_226d17'

def setup_inputs(seed: int=0):
    np.random.seed(seed)
    _w = jnp.asarray

    def _rec_inputs():
        import jax
        import jax.numpy as jnp
        _rk = jax.random.key(seed)
        x = -0.0003929 + 0.9999 * jax.random.normal(jax.random.fold_in(_rk, 1), (32, 128, 128), jnp.float32)
        _lenS = 128 - jax.random.randint(jax.random.fold_in(_rk, 7), (32,), 0, max(1, 128 // 4) + 1, jnp.int32)
        _lenS2 = 77 - jax.random.randint(jax.random.fold_in(_rk, 8), (32,), 0, max(1, 77 // 4) + 1, jnp.int32)
        _ctx_1024P = jax.random.normal(jax.random.fold_in(_rk, 11), (32, 16, 128), jnp.float32)
        _ctx_1024c = jax.random.dirichlet(jax.random.fold_in(_rk, 511), 0.3 * jnp.ones((16,), jnp.float32), (32, 77))
        _ctx_1024t = jnp.einsum('bsk,bkd->bsd', _ctx_1024c, _ctx_1024P)
        _ctx_1024t = _ctx_1024t * jax.lax.rsqrt(jnp.mean(jnp.square(_ctx_1024t)) + 1e-12) * 0.953939
        ctx_1024 = 2.81802e-05 + 1.00001 * (_ctx_1024t + 0.3 * jax.random.normal(jax.random.fold_in(_rk, 611), (32, 77, 128), jnp.float32))
        _g = jax.random.normal(jax.random.fold_in(_rk, 9001), (2, 1), jnp.float32)
        _g = jnp.sign(_g) * jnp.maximum(jnp.abs(_g), 1.0) + (_g == 0) * 1.0
        g_xattn = _g[0]
        g_ffn = _g[1]
        return (x, ctx_1024, g_xattn, g_ffn)
    x, ctx_1024, g_xattn, g_ffn = _rec_inputs()

    def _L0_xattn_setup():
        import jax, jax.numpy as jnp
        import numpy as np
        B, TQ, TV, H = (8, 256, 256, 128)
        LN_EPS = 1e-05
        key = jax.random.key(seed)
        k1, k2, k3, k4 = jax.random.split(key, 4)
        query = jax.random.normal(k1, (B, TQ, H), dtype=jnp.float32)
        value = jax.random.normal(k2, (B, TV, H), dtype=jnp.float32)
        bound = 1.0 / np.sqrt(2 * H)
        W = jax.random.uniform(k3, (H, 2 * H), minval=-bound, maxval=bound, dtype=jnp.float32)
        b = jax.random.uniform(k4, (H,), minval=-bound, maxval=bound, dtype=jnp.float32)
        gamma = jnp.ones((H,), dtype=jnp.float32)
        beta = jnp.zeros((H,), dtype=jnp.float32)
        return {'query': query, 'value': value, 'W': W, 'b': b, 'gamma': gamma, 'beta': beta}
    _L0_xattn_all = _L0_xattn_setup()
    _L0_xattn_in = {k: v for k, v in _L0_xattn_all.items() if k in ('W', 'b', 'gamma', 'beta')}
    del _L0_xattn_all

    def _L0_ffn_setup():
        import jax, jax.numpy as jnp
        import numpy as np
        B, S, H = (4, 256, 128)
        D = 256
        E = 8
        K = 2
        key = jax.random.key(seed)
        ks = jax.random.split(key, 8)
        w = lambda k, shape: jax.random.normal(k, shape, jnp.float32) * 0.02
        return {'hidden_states': jax.random.normal(ks[0], (B, S, H), jnp.float32), 'gate_w': w(ks[1], (H, E)), 'w_gate': w(ks[2], (E, H, D)), 'w_up': w(ks[3], (E, H, D)), 'w_down': w(ks[4], (E, D, H)), 'ws_gate': w(ks[5], (H, D)), 'ws_up': w(ks[6], (H, D)), 'ws_down': w(ks[7], (D, H))}
    _L0_ffn_all = _L0_ffn_setup()
    _L0_ffn_in = {k: v for k, v in _L0_ffn_all.items() if k in ('gate_w', 'w_gate', 'w_up', 'w_down', 'ws_gate', 'ws_up', 'ws_down')}
    del _L0_ffn_all
    return {'x': x, 'ctx_1024': ctx_1024, 'g_xattn': g_xattn, 'g_ffn': g_ffn, 'L0_xattn_W': _L0_xattn_in['W'], 'L0_xattn_b': _L0_xattn_in['b'], 'L0_xattn_gamma': _L0_xattn_in['gamma'], 'L0_xattn_beta': _L0_xattn_in['beta'], 'L0_ffn_gate_w': _L0_ffn_in['gate_w'], 'L0_ffn_w_gate': _L0_ffn_in['w_gate'], 'L0_ffn_w_up': _L0_ffn_in['w_up'], 'L0_ffn_w_down': _L0_ffn_in['w_down'], 'L0_ffn_ws_gate': _L0_ffn_in['ws_gate'], 'L0_ffn_ws_up': _L0_ffn_in['ws_up'], 'L0_ffn_ws_down': _L0_ffn_in['ws_down']}

def reference(x, ctx_1024, g_xattn, g_ffn, L0_xattn_W, L0_xattn_b, L0_xattn_gamma, L0_xattn_beta, L0_ffn_gate_w, L0_ffn_w_gate, L0_ffn_w_up, L0_ffn_w_down, L0_ffn_ws_gate, L0_ffn_ws_up, L0_ffn_ws_down):
    import jax
    import jax.numpy as jnp

    def _L0_xattn_ref(query, value, W, b, gamma, beta):
        import jax, jax.numpy as jnp
        import numpy as np
        B, TQ, TV, H = (8, 256, 256, 128)
        LN_EPS = 1e-05
        score = jnp.einsum('bqh,bvh->bqv', query, value)
        attn = jax.nn.softmax(score, axis=-1)
        context = jnp.einsum('bqv,bvh->bqh', attn, value)
        combined = jnp.concatenate((context, query), axis=2)
        proj = jnp.einsum('bqk,hk->bqh', combined, W) + b
        mean = jnp.mean(proj, axis=-1, keepdims=True)
        var = jnp.mean(jnp.square(proj - mean), axis=-1, keepdims=True)
        out = (proj - mean) * jax.lax.rsqrt(var + LN_EPS) * gamma + beta
        return out

    def _L0_ffn_ref(hidden_states, gate_w, w_gate, w_up, w_down, ws_gate, ws_up, ws_down):
        import jax, jax.numpy as jnp
        import numpy as np
        B, S, H = (4, 256, 128)
        D = 256
        E = 8
        K = 2
        b, s, h = hidden_states.shape
        x = hidden_states.reshape(-1, h)
        scores = jax.nn.softmax(x @ gate_w, axis=-1)
        topk_w, topk_idx = jax.lax.top_k(scores, K)
        topk_w = topk_w / (jnp.sum(topk_w, axis=-1, keepdims=True) + 1e-20)
        onehot = jax.nn.one_hot(topk_idx, E, dtype=x.dtype)
        w_per_expert = jnp.einsum('nke,nk->ne', onehot, topk_w)
        y = jnp.zeros_like(x)
        for e in range(E):
            hid = jax.nn.silu(x @ w_gate[e]) * (x @ w_up[e])
            y = y + w_per_expert[:, e:e + 1] * (hid @ w_down[e])
        shared = jax.nn.silu(x @ ws_gate) * (x @ ws_up) @ ws_down
        return (y + shared).reshape(b, s, h)
    x = x + jnp.tanh(g_xattn[0]) * _L0_xattn_ref(_layernorm(x, axis=-1), ctx_1024, L0_xattn_W, L0_xattn_b, L0_xattn_gamma, L0_xattn_beta)
    x = x + jnp.tanh(g_ffn[0]) * _L0_ffn_ref(_layernorm(x, axis=-1), L0_ffn_gate_w, L0_ffn_w_gate, L0_ffn_w_up, L0_ffn_w_down, L0_ffn_ws_gate, L0_ffn_ws_up, L0_ffn_ws_down)
    return x

_drawn_inputs = setup_inputs


def setup_inputs(seed=0):
    import zlib

    import numpy as np

    out = dict(_drawn_inputs(seed))
    spreads = {'L0_xattn_gamma': (1.0, 0.2), 'L0_xattn_beta': (0.0, 0.1)}
    factors = {'L0_ffn_gate_w': 8.0,
     'L0_ffn_w_gate': 8.0,
     'L0_ffn_w_up': 8.0,
     'L0_ffn_w_down': 8.0,
     'L0_ffn_ws_gate': 8.0,
     'L0_ffn_ws_up': 8.0,
     'L0_ffn_ws_down': 8.0}
    for name, (base, spread) in spreads.items():
        noise = np.random.default_rng([zlib.crc32(name.encode()), seed]).standard_normal(out[name].shape)
        drawn = base * np.exp(spread * noise) if base else spread * noise
        out[name] = jnp.asarray(drawn.astype(out[name].dtype))
    for name, factor in factors.items():
        out[name] = (out[name] * factor).astype(out[name].dtype)
    return out
```

```python
from contextlib import ExitStack

import concourse.bass as bass
from concourse import mybir

ALU = mybir.AluOpType
ACT = mybir.ActivationFunctionType
AX = mybir.AxisListType
F32 = mybir.dt.float32
F16 = mybir.dt.float16

P = 128
LN_EPS = 1e-5
TOPK_EPS = 1e-20
ACT_SCALE = 64.0
W_SCALE = 64.0
HID_SCALE = 4.0


def flamingo_gated_layer(nc, x, ctx_kv, g_xattn, g_ffn, W, b, gamma, beta,
                         gate_w, w_gate, w_up, w_down, ws_gate, ws_up, ws_down, out):
    B, S, H = x.shape
    V = ctx_kv.shape[1]
    E, _, D = w_gate.shape
    assert S == P and H == P and D == 2 * P
    T = 4
    G = B // T
    TH = T * H
    TV = T * V
    NE = E + 1
    C = D // P
    UNITS = C * NE
    NBUF = 3

    with ExitStack() as stack:
        def sb(name, shape, dt=F32):
            return stack.enter_context(nc.sbuf_tensor(name, shape, dt))

        def ps(name, shape):
            return stack.enter_context(nc.psum_tensor(name, shape, F32))

        def sem(name):
            return stack.enter_context(nc.semaphore(name))

        ident = sb("ident", [P, P])
        w_rows = sb("w_rows", [P, 2 * H])
        w_ctx_T = sb("w_ctx_T", [P, H])
        w_qry_T = sb("w_qry_T", [P, H])
        gain = sb("gain", [P, TH])
        shift = sb("shift", [P, TH])
        g_raw = sb("g_raw", [P, 2])
        g_tanh = sb("g_tanh", [P, 2])
        ffn_gain = sb("ffn_gain", [P, 1])
        first_code = sb("first_code", [P, T, E])
        w_f32 = sb("w_f32", [P, NE, 3, D])
        w_hi = sb("w_hi", [P, NE, 3, D], F16)
        w_lo = sb("w_lo", [P, NE, 3, D], F16)
        gw_f32 = sb("gw_f32", [P, E])
        gw_hi = sb("gw_hi", [P, E], F16)
        gw_lo = sb("gw_lo", [P, E], F16)
        x_all = sb("x_all", [P, B * H])
        hT_hi = sb("hT_hi", [P, B * S], F16)
        hT_lo = sb("hT_lo", [P, B * S], F16)
        ctx_in = sb("ctx_in", [V, T, H])
        stats = sb("stats", [P, T, 6])
        mean2 = sb("mean2", [P, T])
        mean = sb("mean", [P, T])
        half_diff = sb("half_diff", [P, T])
        sq_sum = sb("sq_sum", [P, T])
        var_eps = sb("var_eps", [P, T])
        rstd = sb("rstd", [P, T])
        minus_half = sb("minus_half", [P, T])
        xn = sb("xn", [P, TH])
        qT = sb("qT", [P, TH])
        cT = sb("cT", [P, TV])
        neg_max = sb("neg_max", [P, T])
        attn = sb("attn", [P, T, V])
        attn_sum = sb("attn_sum", [P, T])
        attn_rec = sb("attn_rec", [P, T])
        attnT = sb("attnT", [V + 1, TH])
        ctxW = sb("ctxW", [V + 1, TH])
        pn = sb("pn", [P, TH])
        pg = sb("pg", [P, TH])
        xs = sb("xs", [P, TH])
        x1 = sb("x1", [P, TH])
        hn = sb("hn", [P, TH])
        logit = sb("logit", [P, T, E])
        top = sb("top", [P, T])
        code = sb("code", [P, T, E])
        best = sb("best", [P, T])
        one1 = sb("one1", [P, T, E])
        logit2 = sb("logit2", [P, T, E])
        one2 = sb("one2", [P, T, E])
        picked = sb("picked", [P, T, E])
        below_top = sb("below_top", [P, T, E])
        expo = sb("expo", [P, T, E])
        chosen = sb("chosen", [P, T, E])
        sum_all = sb("sum_all", [P, T])
        sum_two = sb("sum_two", [P, T])
        weight = sb("weight", [P, T, E])
        silu = sb("silu", [P, C, TH])
        hid = sb("hid", [P, C, TH])
        hid_hi = sb("hid_hi", [P, NBUF, C, TH], F16)
        hid_lo = sb("hid_lo", [P, NBUF, C, TH], F16)

        gate_ps = [ps(f"gate_ps{c}", [P, TH]) for c in range(C)]
        up_ps = [ps(f"up_ps{c}", [P, TH]) for c in range(C)]
        y_ps = [ps(f"y_ps{i}", [P, TH]) for i in range(2)]
        bank_a = ps("bank_a", [P, 512])
        bank_b = ps("bank_b", [P, 512])

        x_in = sem("x_in")
        x_rest_in = sem("x_rest_in")
        ctx_landed = sem("ctx_landed")
        small_in = sem("small_in")
        w_chunks = [(0, 1), (1, 3), (3, 6), (6, 9)]
        w_in = [sem(f"w_in{i}") for i in range(len(w_chunks))]
        ident_ready = sem("ident_ready")
        consts_ready = sem("consts_ready")
        tanh_ready = sem("tanh_ready")
        gain_ready = sem("gain_ready")
        w_hi_ready = sem("w_hi_ready")
        w_lo_ready = sem("w_lo_ready")
        dve_step = sem("dve_step")
        pool_step = sem("pool_step")
        var_ready = sem("var_ready")
        rstd_ready = sem("rstd_ready")
        xn_ready = sem("xn_ready")
        xT_in_ps = sem("xT_in_ps")
        ctxT_in_ps = sem("ctxT_in_ps")
        qT_ready = sem("qT_ready")
        cT_ready = sem("cT_ready")
        score_in_ps = sem("score_in_ps")
        ctxW_in_ps = sem("ctxW_in_ps")
        max_ready = sem("max_ready")
        ctxW_ready = sem("ctxW_ready")
        exp_ready = sem("exp_ready")
        attn_ready = sem("attn_ready")
        attnT_in_ps = sem("attnT_in_ps")
        attnT_ready = sem("attnT_ready")
        proj_in_ps = sem("proj_in_ps")
        pn_ready = sem("pn_ready")
        x1_ready = sem("x1_ready")
        hn_ready = sem("hn_ready")
        hT_in_ps = sem("hT_in_ps")
        hT_hi_ready = sem("hT_hi_ready")
        hT_lo_ready = sem("hT_lo_ready")
        logit_in_ps = sem("logit_in_ps")
        logit_read = sem("logit_read")
        below_ready = sem("below_ready")
        expo_ready = sem("expo_ready")
        gate_in_ps = sem("gate_in_ps")
        up_in_ps = sem("up_in_ps")
        silu_ready = sem("silu_ready")
        hid_ready = sem("hid_ready")
        hid_hi_ready = sem("hid_hi_ready")
        hid_lo_ready = sem("hid_lo_ready")
        y_in_ps = sem("y_in_ps")
        y_added = sem("y_added")
        stored = sem("stored")

        x_d = x.rearrange("b p h -> p b h")
        out_d = out.rearrange("b p h -> p b h")
        ctx_d = ctx_kv.rearrange("b v h -> v b h")
        x_v = x_all[:, :].rearrange("p (b h) -> p b h", h=H)

        block = stack.enter_context(nc.Block())

        def tile_cols(t, n=H):
            return slice(t * n, (t + 1) * n)

        def parts(t, e):
            return w_hi[:, e, t, :], w_lo[:, e, t, :]

        @block.sync
        def _(sp):
            sp.dma_start(x_v[:, 0:T, :], x_d[:, 0:T, :]).then_inc(x_in, 16)
            sp.dma_start(ctx_in[:, :, :], ctx_d[:, 0:T, :]).then_inc(ctx_landed, 16)
            sp.dma_start(w_rows[:, :], W).then_inc(small_in, 16)
            sp.dma_start(g_raw[:, 0:1], g_xattn.partition_broadcast(P)).then_inc(small_in, 16)
            sp.dma_start(g_raw[:, 1:2], g_ffn.partition_broadcast(P)).then_inc(small_in, 16)
            sp.dma_start(gw_f32[:, :], gate_w).then_inc(small_in, 16)
            for t in range(T):
                sp.dma_start(gain[:, tile_cols(t)], gamma.partition_broadcast(P)).then_inc(small_in, 16)
                sp.dma_start(shift[:, tile_cols(t)], beta.partition_broadcast(P)).then_inc(small_in, 16)
                sp.dma_start(ctxW[V:V + 1, tile_cols(t)], b.unsqueeze(0)).then_inc(small_in, 16)
            sp.dma_start(x_v[:, T:B, :], x_d[:, T:B, :]).then_inc(x_rest_in, 16)

            def load_ctx(a):
                sp.wait_ge(ctxT_in_ps, a)
                sp.dma_start(ctx_in[:, :, :], ctx_d[:, bass.ts(a, T), :]).then_inc(ctx_landed, 16)

            def store(g):
                sp.wait_ge(y_added, 1 + NE * (g + 1))
                sp.dma_start(out_d[:, bass.ts(g, T), :], x_v[:, bass.ts(g, T), :]).then_inc(stored, 16)

            load_ctx(1)
            with sp.Fori(0, G - 2) as g:
                load_ctx(g + 2)
                store(g)
            store(G - 2)
            store(G - 1)
            sp.wait_ge(stored, 16 * G)

        @block.gpsimd
        def _(pool):
            pool.memset(ident[:, :], 0.0).then_inc(pool_step, 1)
            for e in range(E):
                last = pool.memset(first_code[:, :, e:e + 1], float(E - e))
            last.then_inc(consts_ready, 1)
            pool.memset(minus_half[:, :], -0.5).then_inc(consts_ready, 1)
            pool.memset(attnT[:, :], 1.0).then_inc(consts_ready, 1)
            pool.wait_ge(consts_ready, 3)
            pool.wait_ge(pool_step, 1)
            pool.affine_select(out=ident[:, :], in_=ident[:, :], compare_op=ALU.not_equal, fill=1.0,
                               base=0, pattern=[[-1, P]], channel_multiplier=1).then_inc(ident_ready, 1)

            def rstd_pow(a, n):
                pool.wait_ge(var_ready, 3 * a + n + 1)
                pool.tensor_tensor(rstd[:, :], var_eps[:, :], minus_half[:, :], ALU.pow).then_inc(rstd_ready, 1)

            def residual(a):
                k = 1 + 2 * a
                if isinstance(a, int) and a == 0:
                    pool.wait_ge(gain_ready, 2)
                    pool.wait_ge(x_in, 16)
                pool.tensor_tensor(xs[:, :], x_all[:, bass.ts(a, TH)], shift[:, :], ALU.add).then_inc(pool_step, 1)
                pool.wait_ge(pn_ready, a + 1)
                pool.tensor_tensor(pg[:, :], pn[:, :], gain[:, :], ALU.mult).then_inc(pool_step, 1)
                pool.wait_ge(pool_step, k + 2)
                if not (isinstance(a, int) and a == 0):
                    pool.wait_ge(y_added, 1 + NE * (a - 1) + 1)
                pool.tensor_tensor(x1[:, :], xs[:, :], pg[:, :], ALU.add).then_inc(x1_ready, 1)

            def hid_low(g, k, c):
                s = NE * g + k
                u = C * s + c
                pool.wait_ge(hid_hi_ready, u + 1)
                pool.tensor_tensor(hid_lo[:, k % NBUF, c, :], hid[:, c, :], hid_hi[:, k % NBUF, c, :],
                                   ALU.subtract).then_inc(hid_lo_ready, 1)

            rstd_pow(0, 0)
            rstd_pow(0, 1)
            residual(0)
            rstd_pow(0, 2)
            hid_low(0, 0, 0)

            def body(g, last=False):
                for k in range(1, NE if last else NE + 1):
                    hid_low(g, k - 1, 1)
                    if not last:
                        if k == 1:
                            rstd_pow(g + 1, 0)
                        if k == 5:
                            rstd_pow(g + 1, 1)
                        if k == 6:
                            residual(g + 1)
                        if k == 7:
                            rstd_pow(g + 1, 2)
                    hid_low(g, k, 0)
                if last:
                    hid_low(g, NE - 1, 1)

            pool.wait_ge(x_rest_in, 16)
            with pool.Fori(0, G - 1) as g:
                body(g)
            body(G - 1, last=True)

        @block.scalar
        def _(act):
            for n, (lo, hi) in enumerate(w_chunks):
                if lo == 0:
                    act.dma_start(w_f32[:, 0, 0, :], ws_gate).then_inc(w_in[n], 16)
                    act.dma_start(w_f32[:, 0, 1, :], ws_up).then_inc(w_in[n], 16)
                    act.dma_start(w_f32[:, 0, 2, :],
                                  ws_down.rearrange("(p c) h -> p (c h)", c=C)).then_inc(w_in[n], 16)
                else:
                    act.dma_start(w_f32[:, lo:hi, 0, :],
                                  w_gate[lo - 1:hi - 1].rearrange("e h d -> h e d")).then_inc(w_in[n], 16)
                    act.dma_start(w_f32[:, lo:hi, 1, :],
                                  w_up[lo - 1:hi - 1].rearrange("e h d -> h e d")).then_inc(w_in[n], 16)
                    act.dma_start(w_f32[:, lo:hi, 2, :],
                                  w_down[lo - 1:hi - 1].rearrange("e (p c) h -> p e (c h)", c=C)).then_inc(w_in[n], 16)
            act.wait_ge(small_in, 16 * (4 + 3 * T))
            act.activation(g_tanh[:, :], g_raw[:, :], ACT.Tanh).then_inc(tanh_ready, 1)

            def evac_T(a):
                act.wait_ge(xT_in_ps, a + 1)
                if not (isinstance(a, int) and a == 0):
                    act.wait_ge(proj_in_ps, a)
                act.copy(qT[:, :], bank_a[:, :]).then_inc(qT_ready, 1)
                act.wait_ge(ctxT_in_ps, a + 1)
                act.copy(cT[:, :], bank_b[:, 0:TV]).then_inc(cT_ready, 1)

            def softmax_exp(a):
                act.wait_ge(max_ready, a + 1)
                for t in range(T):
                    ins = act.activation(attn[:, t, :], bank_a[:, tile_cols(t, V)], ACT.Exp,
                                         bias=neg_max[:, t:t + 1], accum_out=attn_sum[:, t:t + 1])
                ins.then_inc(exp_ready, 1)

            def evac_attnT(a):
                act.wait_ge(attnT_in_ps, a + 1)
                if isinstance(a, int) and a == 0:
                    act.wait_ge(consts_ready, 3)
                act.copy(attnT[0:V, :], bank_a[0:V, :]).then_inc(attnT_ready, 1)

            def hT_high(a):
                act.wait_ge(hT_in_ps, a + 1)
                act.copy(hT_hi[:, bass.ts(a, TH)], bank_a[:, :]).then_inc(hT_hi_ready, 1)

            def route_exp(a):
                act.wait_ge(below_ready, a + 1)
                act.activation(expo[:, :, :], below_top[:, :, :], ACT.Exp).then_inc(expo_ready, 1)

            def silu_unit(g, k, c):
                s = NE * g + k
                u = C * s + c
                act.wait_ge(gate_in_ps, u + 1)
                if not isinstance(u, int):
                    act.wait_ge(hid_ready, u - 1)
                act.activation(silu[:, c, :], gate_ps[c][:, :], ACT.Silu,
                               scale=1.0 / (ACT_SCALE * W_SCALE)).then_inc(silu_ready, 1)

            def hid_high(g, k, c):
                s = NE * g + k
                u = C * s + c
                act.wait_ge(hid_ready, u + 1)
                if not isinstance(s, int) or s >= NBUF:
                    act.wait_ge(y_in_ps, 1 + NE * g + max(k - NBUF + 1, 0))
                act.copy(hid_hi[:, k % NBUF, c, :], hid[:, c, :]).then_inc(hid_hi_ready, 1)

            evac_T(0)
            act.wait_ge(w_in[0], 48)
            act.mul(w_hi[:, 0, :, :], w_f32[:, 0, :, :], W_SCALE).then_inc(w_hi_ready, 1)
            act.mul(gw_hi[:, :], gw_f32[:, :], W_SCALE).then_inc(w_hi_ready, 1)
            softmax_exp(0)
            evac_attnT(0)
            for n, (lo, hi) in enumerate(w_chunks[1:]):
                act.wait_ge(w_in[n + 1], 48)
                for e in range(lo, hi):
                    act.mul(w_hi[:, e, :, :], w_f32[:, e, :, :], W_SCALE).then_inc(w_hi_ready, 1)
            hT_high(0)
            route_exp(0)
            silu_unit(0, 0, 0)
            silu_unit(0, 0, 1)
            hid_high(0, 0, 0)

            def body(g, last=False):
                for k in range(1, NE if last else NE + 1):
                    silu_unit(g, k, 0)
                    hid_high(g, k - 1, 1)
                    if not last:
                        if k == 2:
                            evac_T(g + 1)
                        if k == 3:
                            softmax_exp(g + 1)
                        if k == 4:
                            evac_attnT(g + 1)
                        if k == 8:
                            hT_high(g + 1)
                    silu_unit(g, k, 1)
                    hid_high(g, k, 0)
                    if k == NE:
                        route_exp(g + 1)
                if last:
                    hid_high(g, NE - 1, 1)

            with act.Fori(0, G - 1) as g:
                body(g)
            body(G - 1, last=True)

        @block.vector
        def _(dve):
            chain = {"base": 0, "n": 0}

            def link(ins):
                chain["n"] += 1
                ins.then_inc(dve_step, 1)
                dve.wait_ge(dve_step, chain["base"] + chain["n"])

            def norm_stats(src, scale=1.0):
                for t in range(T):
                    ins = dve.bn_stats(stats[:, t, :], src(t))
                link(ins)
                m_even, m_odd = stats[:, :, 1], stats[:, :, 4]
                dve.tensor_tensor(mean2[:, :], m_even, m_odd, ALU.add)
                dve.tensor_tensor(half_diff[:, :], m_even, m_odd, ALU.subtract)
                link(dve.tensor_tensor(sq_sum[:, :], stats[:, :, 2], stats[:, :, 5], ALU.add))
                dve.tensor_scalar(mean[:, :], mean2[:, :], 0.5, None, ALU.mult)
                link(dve.tensor_tensor(half_diff[:, :], half_diff[:, :], half_diff[:, :], ALU.mult))
                link(dve.scalar_tensor_tensor(out=sq_sum[:, :], in0=half_diff[:, :], scalar=H / 4,
                                              in1=sq_sum[:, :], op0=ALU.mult, op1=ALU.add))
                dve.tensor_scalar(var_eps[:, :], sq_sum[:, :], 1.0 / (H * scale * scale),
                                  LN_EPS / (scale * scale), ALU.mult, ALU.add).then_inc(var_ready, 1)

            def normalise(dst, src):
                for t in range(T):
                    ins = dve.tensor_scalar(dst[:, tile_cols(t)], src(t), mean[:, t:t + 1],
                                            rstd[:, t:t + 1], ALU.subtract, ALU.mult)
                return ins

            def x_tile(a):
                return lambda t: x_all[:, bass.ds(a * TH + t * H, H)]

            def norm_x(a):
                dve.wait_ge(rstd_ready, 3 * a + 1)
                if not (isinstance(a, int) and a == 0):
                    dve.wait_ge(xT_in_ps, a)
                normalise(xn, x_tile(a)).then_inc(xn_ready, 1)

            def row_max(a):
                dve.wait_ge(score_in_ps, a + 1)
                dve.tensor_reduce(neg_max[:, :], bank_a[:, 0:TV].rearrange("p (t v) -> p t v", v=V),
                                  AX.X, ALU.max, negate=True).then_inc(max_ready, 1)

            def evac_ctxW(a):
                dve.wait_ge(ctxW_in_ps, a + 1)
                dve.tensor_copy(ctxW[0:V, :], bank_b[0:V, :]).then_inc(ctxW_ready, 1)

            def attn_div(a):
                dve.wait_ge(exp_ready, a + 1)
                link(dve.reciprocal(attn_rec[:, :], attn_sum[:, :]))
                for t in range(T):
                    ins = dve.tensor_scalar(attn[:, t, :], attn[:, t, :], attn_rec[:, t:t + 1], None, ALU.mult)
                ins.then_inc(attn_ready, 1)

            def proj_tile(t):
                return bank_b[:, tile_cols(t)]

            def x1_tile(t):
                return x1[:, tile_cols(t)]

            def stats_proj(a):
                dve.wait_ge(proj_in_ps, a + 1)
                norm_stats(proj_tile)

            def norm_proj(a):
                dve.wait_ge(rstd_ready, 3 * a + 2)
                normalise(pn, proj_tile).then_inc(pn_ready, 1)

            def stats_x1(a):
                dve.wait_ge(x1_ready, a + 1)
                norm_stats(x1_tile, ACT_SCALE)

            def norm_x1(a):
                dve.wait_ge(rstd_ready, 3 * a + 3)
                if not (isinstance(a, int) and a == 0):
                    dve.wait_ge(hT_in_ps, a)
                normalise(hn, x1_tile).then_inc(hn_ready, 1)

            def hT_low(a):
                dve.wait_ge(hT_hi_ready, a + 1)
                cols = bass.ts(a, TH)
                dve.tensor_tensor(hT_lo[:, cols], bank_a[:, :], hT_hi[:, cols],
                                  ALU.subtract).then_inc(hT_lo_ready, 1)

            def over(v):
                return v[:, :].unsqueeze(2).to_broadcast([P, T, E])

            def route_pick(a):
                dve.wait_ge(logit_in_ps, a + 1)
                dve.tensor_scalar(logit[:, :, :], bank_b[:, 0:T * E].rearrange("p (t e) -> p t e", e=E),
                                  1.0 / (ACT_SCALE * W_SCALE), None, ALU.mult).then_inc(logit_read, 1)
                dve.wait_ge(logit_read, a + 1)
                link(dve.tensor_reduce(top[:, :], logit[:, :, :], AX.X, ALU.max))
                dve.tensor_tensor(below_top[:, :, :], logit[:, :, :], over(top),
                                  ALU.subtract).then_inc(below_ready, 1)
                link(dve.tensor_tensor(code[:, :, :], logit[:, :, :], over(top), ALU.is_ge))
                link(dve.tensor_tensor(code[:, :, :], code[:, :, :], first_code[:, :, :], ALU.mult))
                link(dve.tensor_reduce(best[:, :], code[:, :, :], AX.X, ALU.max))
                link(dve.tensor_tensor(one1[:, :, :], first_code[:, :, :], over(best), ALU.is_equal))
                link(dve.scalar_tensor_tensor(out=logit2[:, :, :], in0=one1[:, :, :], scalar=-1e30,
                                              in1=logit[:, :, :], op0=ALU.mult, op1=ALU.add))
                link(dve.tensor_reduce(top[:, :], logit2[:, :, :], AX.X, ALU.max))
                link(dve.tensor_tensor(code[:, :, :], logit2[:, :, :], over(top), ALU.is_ge))
                link(dve.tensor_tensor(code[:, :, :], code[:, :, :], first_code[:, :, :], ALU.mult))
                link(dve.tensor_reduce(best[:, :], code[:, :, :], AX.X, ALU.max))
                link(dve.tensor_tensor(one2[:, :, :], first_code[:, :, :], over(best), ALU.is_equal))
                link(dve.tensor_tensor(picked[:, :, :], one1[:, :, :], one2[:, :, :], ALU.add))

            def route_weights(a):
                dve.wait_ge(expo_ready, a + 1)
                dve.tensor_reduce(sum_all[:, :], expo[:, :, :], AX.X, ALU.add)
                link(dve.tensor_tensor(chosen[:, :, :], expo[:, :, :], picked[:, :, :], ALU.mult))
                link(dve.tensor_reduce(sum_two[:, :], chosen[:, :, :], AX.X, ALU.add))
                link(dve.scalar_tensor_tensor(out=sum_two[:, :], in0=sum_all[:, :], scalar=TOPK_EPS,
                                              in1=sum_two[:, :], op0=ALU.mult, op1=ALU.add))
                link(dve.reciprocal(sum_two[:, :], sum_two[:, :]))
                link(dve.tensor_scalar(sum_two[:, :], sum_two[:, :], ffn_gain[:, 0:1], None, ALU.mult))
                link(dve.tensor_tensor(weight[:, :, :], chosen[:, :, :], over(sum_two), ALU.mult))

            def hid_unit(g, k, c):
                s = NE * g + k
                u = C * s + c
                dve.wait_ge(up_in_ps, u + 1)
                dve.wait_ge(silu_ready, u + 1)
                if not isinstance(u, int) or u >= C:
                    dve.wait_ge(hid_lo_ready, u - 1)
                dve.scalar_tensor_tensor(out=hid[:, c, :], in0=up_ps[c][:, :],
                                         scalar=HID_SCALE / (ACT_SCALE * W_SCALE), in1=silu[:, c, :],
                                         op0=ALU.mult, op1=ALU.mult).then_inc(hid_ready, 1)

            def add_y(g, k):
                s = NE * g + k
                dve.wait_ge(y_in_ps, 1 + s + 1)
                dve.wait_ge(y_added, 1 + s)
                if k == 0:
                    ins = dve.scalar_tensor_tensor(out=x_all[:, bass.ts(g, TH)], in0=y_ps[0][:, :],
                                                   scalar=ffn_gain[:, 0:1], in1=x1[:, :], op0=ALU.mult, op1=ALU.add)
                else:
                    for t in range(T):
                        xt = x_tile(g)(t)
                        ins = dve.scalar_tensor_tensor(out=xt, in0=y_ps[k % 2][:, tile_cols(t)],
                                                       scalar=weight[:, t, k - 1:k], in1=xt,
                                                       op0=ALU.mult, op1=ALU.add)
                ins.then_inc(y_added, 1)

            dve.wait_ge(x_in, 16)
            norm_stats(x_tile(0))
            norm_x(0)
            dve.wait_ge(tanh_ready, 1)
            dve.tensor_scalar(gain[:, :], gain[:, :], g_tanh[:, 0:1], None, ALU.mult).then_inc(gain_ready, 1)
            dve.tensor_scalar(shift[:, :], shift[:, :], g_tanh[:, 0:1], None, ALU.mult).then_inc(gain_ready, 1)
            link(dve.tensor_scalar(ffn_gain[:, :], g_tanh[:, 1:2], 1.0 / (HID_SCALE * W_SCALE), None, ALU.mult))
            dve.wait_ge(y_in_ps, 1)
            dve.tensor_copy(w_ctx_T[:, :], y_ps[0][:, 0:H])
            dve.tensor_copy(w_qry_T[:, :], y_ps[0][:, H:2 * H]).then_inc(y_added, 1)

            def weight_low(dst, src, high, n):
                dve.wait_ge(w_hi_ready, n)
                return dve.scalar_tensor_tensor(out=dst, in0=src, scalar=W_SCALE, in1=high,
                                                op0=ALU.mult, op1=ALU.subtract)

            weight_low(w_lo[:, 0, :, :].rearrange("p a d -> p (a d)"), w_f32[:, 0, :, :].rearrange("p a d -> p (a d)"),
                       w_hi[:, 0, :, :].rearrange("p a d -> p (a d)"), 1).then_inc(w_lo_ready, 1)
            weight_low(gw_lo[:, :], gw_f32[:, :], gw_hi[:, :], 2).then_inc(w_lo_ready, 1)
            row_max(0)
            evac_ctxW(0)
            attn_div(0)
            stats_proj(0)
            norm_proj(0)
            stats_x1(0)
            norm_x1(0)
            for e in range(1, NE):
                weight_low(w_lo[:, e, :, :].rearrange("p a d -> p (a d)"),
                           w_f32[:, e, :, :].rearrange("p a d -> p (a d)"),
                           w_hi[:, e, :, :].rearrange("p a d -> p (a d)"), 2 + e).then_inc(w_lo_ready, 1)
            hT_low(0)
            route_pick(0)
            dve.wait_ge(x_rest_in, 16)
            hid_unit(0, 0, 0)
            hid_unit(0, 0, 1)

            def body(g, last=False):
                for k in range(1, NE if last else NE + 1):
                    if k == 1:
                        route_weights(g)
                    hid_unit(g, k, 0)
                    if not last:
                        if k == 1:
                            norm_stats(x_tile(g + 1))
                        if k == 3:
                            row_max(g + 1)
                            evac_ctxW(g + 1)
                        if k == 4:
                            attn_div(g + 1)
                        if k == 5:
                            stats_proj(g + 1)
                        if k == 7:
                            stats_x1(g + 1)
                        if k == 8:
                            hT_low(g + 1)
                    hid_unit(g, k, 1)
                    if not last:
                        if k == 1:
                            norm_x(g + 1)
                        if k == 5:
                            norm_proj(g + 1)
                        if k == 7:
                            norm_x1(g + 1)
                    add_y(g, k - 1)
                    if k == NE:
                        route_pick(g + 1)
                if last:
                    add_y(g, NE - 1)

            before = chain["n"]
            per_body = 31
            with dve.Fori(0, G - 1) as g:
                chain["base"], chain["n"] = before + g * per_body, 0
                body(g)
                assert chain["n"] == per_body, chain["n"]
            chain["base"], chain["n"] = before + (G - 1) * per_body, 0
            body(G - 1, last=True)

        @block.tensor
        def _(pe):
            def transpose_in(a):
                pe.wait_ge(xn_ready, a + 1)
                if not (isinstance(a, int) and a == 0):
                    pe.wait_ge(hT_lo_ready, a)
                for t in range(T):
                    ins = pe.transpose(bank_a[:, tile_cols(t)], xn[:, tile_cols(t)], ident[:, :])
                ins.then_inc(xT_in_ps, 1)
                pe.wait_ge(ctx_landed, 16 * (a + 1))
                if not (isinstance(a, int) and a == 0):
                    pe.wait_ge(logit_read, a)
                for t in range(T):
                    ins = pe.transpose(bank_b[:, tile_cols(t, V)], ctx_in[:, t, :], ident[0:V, 0:V])
                ins.then_inc(ctxT_in_ps, 1)

            def scores(a):
                pe.wait_ge(qT_ready, a + 1)
                pe.wait_ge(cT_ready, a + 1)
                for t in range(T):
                    ins = pe.matmul(bank_a[:, tile_cols(t, V)], qT[:, tile_cols(t)], cT[:, tile_cols(t, V)],
                                    start=True, stop=True)
                ins.then_inc(score_in_ps, 1)
                for t in range(T):
                    ins = pe.matmul(bank_b[0:V, tile_cols(t)], cT[:, tile_cols(t, V)], w_ctx_T[:, :],
                                    start=True, stop=True)
                ins.then_inc(ctxW_in_ps, 1)

            def transpose_attn(a):
                pe.wait_ge(attn_ready, a + 1)
                for t in range(T):
                    ins = pe.transpose(bank_a[0:V, tile_cols(t)], attn[:, t, :], ident[:, :])
                ins.then_inc(attnT_in_ps, 1)

            def project(a):
                pe.wait_ge(attnT_ready, a + 1)
                pe.wait_ge(ctxW_ready, a + 1)
                for t in range(T):
                    pe.matmul(bank_b[:, tile_cols(t)], attnT[:, tile_cols(t)], ctxW[:, tile_cols(t)],
                              start=True, stop=False)
                    ins = pe.matmul(bank_b[:, tile_cols(t)], qT[:, tile_cols(t)], w_qry_T[:, :],
                                    start=False, stop=True)
                ins.then_inc(proj_in_ps, 1)

            def transpose_h(a):
                pe.wait_ge(hn_ready, a + 1)
                for t in range(T):
                    ins = pe.transpose(bank_a[:, tile_cols(t)], hn[:, tile_cols(t)], ident[:, :])
                ins.then_inc(hT_in_ps, 1)

            def route_logits(a):
                pe.wait_ge(hT_lo_ready, a + 1)
                for t in range(T):
                    cols = bass.ds(a * TH + t * S, S)
                    o = bank_b[:, tile_cols(t, E)]
                    pe.matmul(o, hT_hi[:, cols], gw_hi[:, :], start=True, stop=False)
                    pe.matmul(o, hT_hi[:, cols], gw_lo[:, :], start=False, stop=False)
                    ins = pe.matmul(o, hT_lo[:, cols], gw_hi[:, :], start=False, stop=True)
                ins.then_inc(logit_in_ps, 1)

            def gate_up(g, k, c):
                s = NE * g + k
                u = C * s + c
                cols = bass.ts(g + 1 if k == NE else g, TH)
                if k == NE and c == 0:
                    pe.wait_ge(hT_lo_ready, g + 2)
                e = k % NE
                for part, bank, free, done in ((0, gate_ps[c], silu_ready, gate_in_ps),
                                               (1, up_ps[c], hid_ready, up_in_ps)):
                    wh, wl = parts(part, e)
                    if not isinstance(u, int) or u >= C:
                        pe.wait_ge(free, u - 1)
                    pe.matmul(bank[:, :], wh[:, c:D:C], hT_hi[:, cols], start=True, stop=False)
                    pe.matmul(bank[:, :], wh[:, c:D:C], hT_lo[:, cols], start=False, stop=False)
                    pe.matmul(bank[:, :], wl[:, c:D:C], hT_hi[:, cols], start=False,
                              stop=True).then_inc(done, 1)

            def down(g, k):
                s = NE * g + k
                wh, wl = parts(2, k)
                o = y_ps[k % 2]
                pe.wait_ge(hid_lo_ready, C * (s + 1))
                pe.wait_ge(y_added, 1 + (s if k == 0 else s - 1))
                for t in range(T):
                    for c in range(C):
                        hh = hid_hi[:, k % NBUF, c, tile_cols(t)]
                        hl = hid_lo[:, k % NBUF, c, tile_cols(t)]
                        pe.matmul(o[:, tile_cols(t)], hh, wh[:, tile_cols(c, P)], start=(c == 0), stop=False)
                        pe.matmul(o[:, tile_cols(t)], hh, wl[:, tile_cols(c, P)], start=False, stop=False)
                        ins = pe.matmul(o[:, tile_cols(t)], hl, wh[:, tile_cols(c, P)], start=False,
                                        stop=(c == C - 1))
                ins.then_inc(y_in_ps, 1)

            pe.wait_ge(ident_ready, 1)
            pe.wait_ge(small_in, 16 * (4 + 3 * T))
            pe.transpose(y_ps[0][:, 0:H], w_rows[:, 0:H], ident[:, :])
            pe.transpose(y_ps[0][:, H:2 * H], w_rows[:, H:2 * H], ident[:, :]).then_inc(y_in_ps, 1)
            transpose_in(0)
            pe.wait_ge(y_added, 1)
            scores(0)
            transpose_attn(0)
            project(0)
            transpose_h(0)
            pe.wait_ge(w_lo_ready, 1 + NE)
            route_logits(0)
            gate_up(0, 0, 0)
            gate_up(0, 0, 1)

            def body(g, last=False):
                for k in range(1, NE if last else NE + 1):
                    gate_up(g, k, 0)
                    if not last:
                        if k == 2:
                            transpose_in(g + 1)
                        if k == 3:
                            scores(g + 1)
                        if k == 4:
                            transpose_attn(g + 1)
                        if k == 5:
                            project(g + 1)
                        if k == 8:
                            transpose_h(g + 1)
                        if k == 9:
                            route_logits(g + 1)
                    gate_up(g, k, 1)
                    down(g, k - 1)
                if last:
                    down(g, NE - 1)

            with pe.Fori(0, G - 1) as g:
                body(g)
            body(G - 1, last=True)


_INS = ["x", "ctx_1024", "g_xattn", "g_ffn", "L0_xattn_W", "L0_xattn_b", "L0_xattn_gamma", "L0_xattn_beta",
        "L0_ffn_gate_w", "L0_ffn_w_gate", "L0_ffn_w_up", "L0_ffn_w_down", "L0_ffn_ws_gate", "L0_ffn_ws_up",
        "L0_ffn_ws_down"]


def kernel(**inputs):
    import numpy as _np
    import concourse.bacc as _bacc
    from concourse import mybir as _mybir
    from concourse.bass_utils import run_bass_kernel_spmd as _run

    nc = _bacc.Bacc("TRN2", target_bir_lowering=False, num_devices=1)
    arrays, args = {}, []
    for name in _INS:
        a = _np.ascontiguousarray(inputs[name])
        arrays[f"in_{name}"] = a
        args.append(nc.dram_tensor(f"in_{name}", a.shape, _mybir.dt.from_np(a.dtype), kind="ExternalInput").ap())
    shape = inputs["x"].shape
    args.append(nc.dram_tensor("out_0", shape, _mybir.dt.float32, kind="ExternalOutput").ap())
    flamingo_gated_layer(nc, *args)
    r = _run(nc, [arrays], core_ids=[0])
    return r.results[0]["out_0"]
```

```python
from contextlib import ExitStack

import concourse.bass as bass
from concourse import mybir

ALU = mybir.AluOpType
ACT = mybir.ActivationFunctionType
AX = mybir.AxisListType
F32 = mybir.dt.float32
F16 = mybir.dt.float16

P = 128
LN_EPS = 1e-5
TOPK_EPS = 1e-20
ACT_SCALE = 64.0
W_SCALE = 64.0
HID_SCALE = 4.0


def flamingo_gated_layer(nc, x, ctx_kv, g_xattn, g_ffn, W, b, gamma, beta,
                         gate_w, w_gate, w_up, w_down, ws_gate, ws_up, ws_down, out):
    B, S, H = x.shape
    V = ctx_kv.shape[1]
    E, _, D = w_gate.shape
    assert S == P and H == P and D == 2 * P
    T = 4
    G = B // T
    TH = T * H
    TV = T * V
    NE = E + 1
    C = D // P
    UNITS = C * NE
    NBUF = 3
    UBUF = 3
    LAG = 2
    assert NE % NBUF == 0 and UNITS % UBUF == 0

    with ExitStack() as stack:
        def sb(name, shape, dt=F32):
            return stack.enter_context(nc.sbuf_tensor(name, shape, dt))

        def ps(name, shape):
            return stack.enter_context(nc.psum_tensor(name, shape, F32))

        def sem(name):
            return stack.enter_context(nc.semaphore(name))

        ident = sb("ident", [P, P])
        w_rows = sb("w_rows", [P, 2 * H])
        w_ctx_T = sb("w_ctx_T", [P, H])
        w_qry_T = sb("w_qry_T", [P, H])
        gain = sb("gain", [P, TH])
        shift = sb("shift", [P, TH])
        g_raw = sb("g_raw", [P, 2])
        g_tanh = sb("g_tanh", [P, 2])
        ffn_gain = sb("ffn_gain", [P, 1])
        first_code = sb("first_code", [P, T, E])
        w_f32 = sb("w_f32", [P, NE, 3, D])
        w_hi = sb("w_hi", [P, NE, 3, D], F16)
        w_lo = sb("w_lo", [P, NE, 3, D], F16)
        gw_f32 = sb("gw_f32", [P, E])
        gw_hi = sb("gw_hi", [P, E], F16)
        gw_lo = sb("gw_lo", [P, E], F16)
        x_all = sb("x_all", [P, B * H])
        expd = sb("expd", [P, B * V])
        expd_sum = sb("expd_sum", [P, B])
        query_W = sb("query_W", [P, B * H])
        ctxW = sb("ctxW", [V + 1, B * H])
        hT_hi = sb("hT_hi", [P, B * S], F16)
        hT_lo = sb("hT_lo", [P, B * S], F16)
        stats = sb("stats", [P, B, 6])
        mean2 = sb("mean2", [P, B])
        mean = sb("mean", [P, T])
        mean_x = sb("mean_x", [P, B])
        half_diff = sb("half_diff", [P, B])
        sq_sum = sb("sq_sum", [P, B])
        var_x = sb("var_x", [P, B])
        rstd_x = sb("rstd_x", [P, B])
        var_eps = sb("var_eps", [P, T])
        rstd = sb("rstd", [P, T])
        minus_half = sb("minus_half", [P, B])
        ctx_in = sb("ctx_in", [V, T, H])
        xn = sb("xn", [P, TH])
        qT = sb("qT", [P, TH])
        cT = sb("cT", [P, TV])
        neg_max = sb("neg_max", [P, T])
        attn = sb("attn", [P, T, V])
        attn_rec = sb("attn_rec", [P, T])
        attnT = sb("attnT", [V + 1, TH])
        proj = sb("proj", [P, TH])
        pn = sb("pn", [P, TH])
        pg = sb("pg", [P, TH])
        xs = sb("xs", [P, TH])
        x1 = sb("x1", [P, TH])
        hn = sb("hn", [P, TH])
        logit = sb("logit", [P, T, E])
        top = sb("top", [P, T])
        code = sb("code", [P, T, E])
        best = sb("best", [P, T])
        one1 = sb("one1", [P, T, E])
        logit2 = sb("logit2", [P, T, E])
        one2 = sb("one2", [P, T, E])
        picked = sb("picked", [P, T, E])
        below_top = sb("below_top", [P, T, E])
        euler = sb("euler", [P, T, E])
        expo = sb("expo", [P, T, E])
        chosen = sb("chosen", [P, T, E])
        sum_all = sb("sum_all", [P, T])
        sum_two = sb("sum_two", [P, T])
        weight = sb("weight", [P, T, E])
        silu = sb("silu", [P, UBUF, TH])
        hid = sb("hid", [P, UBUF, TH])
        hid_hi = sb("hid_hi", [P, NBUF, C, TH], F16)
        hid_lo = sb("hid_lo", [P, NBUF, C, TH], F16)

        gate_ps = [ps(f"gate_ps{c}", [P, TH]) for c in range(C)]
        up_ps = [ps(f"up_ps{c}", [P, TH]) for c in range(C)]
        y_ps = [ps(f"y_ps{i}", [P, TH]) for i in range(2)]
        bank_a = ps("bank_a", [P, 512])
        bank_b = ps("bank_b", [P, 512])
        score_ps, ctxW_ps, query_ps, w_T_ps = y_ps[0], y_ps[1], gate_ps[0], up_ps[0]

        x_parts = [(0, T), (T, 4 * T), (4 * T, B)]
        x_in = [sem(f"x_in{i}") for i in range(len(x_parts))]
        ctx_landed = sem("ctx_landed")
        small_in = sem("small_in")
        N_SMALL = 5 + 2 * T
        w_chunks = [(0, 1), (1, 3), (3, 6), (6, 9)]
        w_in = [sem(f"w_in{i}") for i in range(len(w_chunks))]
        ident_ready = sem("ident_ready")
        consts_ready = sem("consts_ready")
        tanh_ready = sem("tanh_ready")
        gain_ready = sem("gain_ready")
        w_scaled = sem("w_scaled")
        w_hi_ready = sem("w_hi_ready")
        w_lo_ready = sem("w_lo_ready")
        gw_hi_ready = sem("gw_hi_ready")
        gw_ready = sem("gw_ready")
        dve_step = sem("dve_step")
        pool_step = sem("pool_step")
        var_ready = sem("var_ready")
        rstd_ready = sem("rstd_ready")
        xn_ready = sem("xn_ready")
        xT_in_ps = sem("xT_in_ps")
        ctxT_in_ps = sem("ctxT_in_ps")
        qT_ready = sem("qT_ready")
        cT_ready = sem("cT_ready")
        score_in_ps = sem("score_in_ps")
        query_in_ps = sem("query_in_ps")
        ctxW_in_ps = sem("ctxW_in_ps")
        max_ready = sem("max_ready")
        exp_ready = sem("exp_ready")
        query_ready = sem("query_ready")
        ctxW_ready = sem("ctxW_ready")
        attn_ready = sem("attn_ready")
        attnT_in_ps = sem("attnT_in_ps")
        attnT_ready = sem("attnT_ready")
        proj_in_ps = sem("proj_in_ps")
        pn_ready = sem("pn_ready")
        x1_ready = sem("x1_ready")
        hn_ready = sem("hn_ready")
        hT_in_ps = sem("hT_in_ps")
        hT_hi_ready = sem("hT_hi_ready")
        hT_lo_ready = sem("hT_lo_ready")
        logit_in_ps = sem("logit_in_ps")
        logit_read = sem("logit_read")
        below_ready = sem("below_ready")
        expo_ready = sem("expo_ready")
        gate_in_ps = sem("gate_in_ps")
        up_in_ps = sem("up_in_ps")
        silu_ready = sem("silu_ready")
        hid_ready = sem("hid_ready")
        hid_hi_ready = sem("hid_hi_ready")
        hid_lo_ready = sem("hid_lo_ready")
        y_in_ps = sem("y_in_ps")
        y_added = sem("y_added")
        stored = sem("stored")

        x_d = x.rearrange("b p h -> p b h")
        out_d = out.rearrange("b p h -> p b h")
        ctx_d = ctx_kv.rearrange("b v h -> v b h")
        w_f32_flat = w_f32[:, :, :, :].rearrange("p e a d -> p (e a d)")
        w_hi_flat = w_hi[:, :, :, :].rearrange("p e a d -> p (e a d)")
        assert G == NE - 1
        x_v = x_all[:, :].rearrange("p (b h) -> p b h", h=H)

        block = stack.enter_context(nc.Block())

        NX = len(x_parts)

        def norm_count(a, n):
            return NX + 2 * a + n + 1

        def is_first(a):
            return isinstance(a, int) and a == 0

        def tile_cols(t, n=H):
            return slice(t * n, (t + 1) * n)

        def parts(t, e):
            return w_hi[:, e, t, :], w_lo[:, e, t, :]

        @block.sync
        def _(sp):
            def load_x(n):
                lo, hi = x_parts[n]
                sp.dma_start(x_v[:, lo:hi, :], x_d[:, lo:hi, :]).then_inc(x_in[n], 16)

            def load_weights(n):
                lo, hi = w_chunks[n]
                if lo == 0:
                    loads = ((0, ws_gate), (1, ws_up), (2, ws_down.rearrange("(p c) h -> p (c h)", c=C)))
                    for part, src in loads:
                        sp.dma_start(w_f32[:, 0, part, :], src).then_inc(w_in[n], 16)
                    return
                loads = ((0, w_gate, "e h d -> h e d"), (1, w_up, "e h d -> h e d"),
                         (2, w_down, "e (p c) h -> p e (c h)"))
                for part, src, order in loads:
                    sizes = {"c": C} if part == 2 else {}
                    sp.dma_start(w_f32[:, lo:hi, part, :],
                                 src[lo - 1:hi - 1].rearrange(order, **sizes)).then_inc(w_in[n], 16)

            load_x(0)
            sp.dma_start(ctx_in[:, :, :], ctx_d[:, 0:T, :]).then_inc(ctx_landed, 16)
            load_x(1)
            load_x(2)
            for n in range(len(w_chunks)):
                load_weights(n)
            with sp.Fori(1, G) as a:
                sp.wait_ge(ctxT_in_ps, a)
                sp.dma_start(ctx_in[:, :, :], ctx_d[:, bass.ts(a, T), :]).then_inc(ctx_landed, 16)

            def store(g):
                sp.wait_ge(y_added, 1 + NE * (g + 1))
                sp.dma_start(out_d[:, bass.ts(g, T), :], x_v[:, bass.ts(g, T), :]).then_inc(stored, 16)

            with sp.Fori(0, G) as g:
                store(g)
            sp.wait_ge(stored, 16 * G)

        @block.gpsimd
        def _(pool):
            pool.memset(ident[:, :], 0.0).then_inc(pool_step, 1)
            pool.memset(minus_half[:, :], -0.5).then_inc(consts_ready, 1)
            pool.wait_ge(pool_step, 1)
            pool.affine_select(out=ident[:, :], in_=ident[:, :], compare_op=ALU.not_equal, fill=1.0,
                               base=0, pattern=[[-1, P]], channel_multiplier=1).then_inc(ident_ready, 1)
            pool.memset(attnT[:, :], 1.0).then_inc(consts_ready, 1)
            for e in range(E):
                last = pool.memset(first_code[:, :, e:e + 1], float(E - e))
            last.then_inc(consts_ready, 1)
            pool.memset(euler[:, :, :], 2.718281828459045).then_inc(consts_ready, 1)
            pool.wait_ge(consts_ready, 4)

            def power(dst, src, n, count):
                pool.wait_ge(var_ready, count)
                pool.tensor_tensor(dst, src, minus_half[:, 0:n], ALU.pow).then_inc(rstd_ready, 1)

            def rstd_pow(a, n):
                power(rstd[:, :], var_eps[:, :], T, norm_count(a, n))

            def shifted(a):
                pool.tensor_tensor(xs[:, :], x_all[:, bass.ts(a, TH)], shift[:, :], ALU.add).then_inc(pool_step, 1)

            def residual(a):
                pool.wait_ge(pn_ready, a + 1)
                pool.tensor_tensor(pg[:, :], pn[:, :], gain[:, :], ALU.mult).then_inc(pool_step, 1)
                pool.wait_ge(pool_step, 3 + 2 * a)
                if not is_first(a):
                    pool.wait_ge(y_added, 1 + NE * (a - 1) + 1)
                pool.tensor_tensor(x1[:, :], xs[:, :], pg[:, :], ALU.add).then_inc(x1_ready, 1)

            def route_exp(a):
                pool.wait_ge(below_ready, a + 1)
                pool.tensor_tensor(expo[:, :, :], euler[:, :, :], below_top[:, :, :], ALU.pow).then_inc(expo_ready, 1)

            def hid_low(g, k, c):
                s = NE * g + k
                u = C * s + c
                pool.wait_ge(hid_hi_ready, u + 1)
                pool.tensor_tensor(hid_lo[:, k % NBUF, c, :], hid[:, (C * k + c) % UBUF, :],
                                   hid_hi[:, k % NBUF, c, :], ALU.subtract).then_inc(hid_lo_ready, 1)

            def scale_weights(e):
                for n, (lo, _) in enumerate(w_chunks):
                    if e == lo:
                        pool.wait_ge(w_in[n], 48)
                flat = w_f32[:, e, :, :].rearrange("p a d -> p (a d)")
                pool.tensor_scalar(flat, flat, W_SCALE, 1.0, ALU.mult, ALU.mult).then_inc(w_scaled, 1)

            def weight_low(e):
                pool.wait_ge(w_hi_ready, e + 1)
                pool.tensor_tensor(w_lo[:, e, :, :].rearrange("p a d -> p (a d)"),
                                   w_f32[:, e, :, :].rearrange("p a d -> p (a d)"),
                                   w_hi[:, e, :, :].rearrange("p a d -> p (a d)"),
                                   ALU.subtract).then_inc(w_lo_ready, 1)

            for n, (lo, hi) in enumerate(x_parts):
                power(rstd_x[:, lo:hi], var_x[:, lo:hi], hi - lo, n + 1)
            scale_weights(0)
            for e in range(1, NE):
                scale_weights(e)
                weight_low(e - 1)
            weight_low(NE - 1)
            pool.wait_ge(gain_ready, 2)
            shifted(0)
            rstd_pow(0, 0)
            residual(0)
            rstd_pow(0, 1)
            route_exp(0)
            hid_low(0, 0, 0)
            hid_low(0, 0, 1)
            hid_low(0, 1, 0)

            def body(g, last=False):
                for k in range(LAG, NE if last else NE + LAG):
                    hid_low(g, k - 1, 1)
                    if not last:
                        if k == 5:
                            rstd_pow(g + 1, 0)
                        if k == 7:
                            rstd_pow(g + 1, 1)
                        if k == 10:
                            route_exp(g + 1)
                    hid_low(g, k, 0)
                    if not last:
                        if k == 3:
                            shifted(g + 1)
                        if k == 5:
                            residual(g + 1)
                if last:
                    hid_low(g, NE - 1, 1)

            with pool.Fori(0, G - 1) as g:
                body(g)
            body(G - 1, last=True)

        @block.scalar
        def _(act):
            act.dma_start(w_rows[:, :], W).then_inc(small_in, 16)
            act.dma_start(g_raw[:, 0:1], g_xattn.partition_broadcast(P)).then_inc(small_in, 16)
            act.dma_start(g_raw[:, 1:2], g_ffn.partition_broadcast(P)).then_inc(small_in, 16)
            act.dma_start(gw_f32[:, :], gate_w).then_inc(small_in, 16)
            for t in range(T):
                act.dma_start(gain[:, tile_cols(t)], gamma.partition_broadcast(P)).then_inc(small_in, 16)
                act.dma_start(shift[:, tile_cols(t)], beta.partition_broadcast(P)).then_inc(small_in, 16)
            act.dma_start(ctxW[V:V + 1, :].rearrange("o (b h) -> o b h", h=H),
                          b.unsqueeze(0).unsqueeze(0).to_broadcast([1, B, H])).then_inc(small_in, 16)
            act.wait_ge(small_in, 16 * N_SMALL)
            act.activation(g_tanh[:, :], g_raw[:, :], ACT.Tanh).then_inc(tanh_ready, 1)
            act.mul(gw_hi[:, :], gw_f32[:, :], W_SCALE).then_inc(gw_hi_ready, 1)

            def evac_qT(a):
                act.wait_ge(xT_in_ps, a + 1)
                if not is_first(a):
                    act.wait_ge(query_in_ps, a)
                act.copy(qT[:, :], bank_a[:, :]).then_inc(qT_ready, 1)

            def evac_cT(a):
                act.wait_ge(ctxT_in_ps, a + 1)
                if not is_first(a):
                    act.wait_ge(ctxW_in_ps, a)
                act.copy(cT[:, :], bank_b[:, 0:TV]).then_inc(cT_ready, 1)

            def softmax_exp(a):
                act.wait_ge(max_ready, a + 1)
                for t in range(T):
                    ins = act.activation(expd[:, bass.ds(a * TV + t * V, V)], score_ps[:, tile_cols(t, V)],
                                         ACT.Exp, bias=neg_max[:, t:t + 1],
                                         accum_out=expd_sum[:, bass.ds(a * T + t, 1)])
                ins.then_inc(exp_ready, 1)

            def evac_query(a):
                act.wait_ge(query_in_ps, a + 1)
                act.copy(query_W[:, bass.ts(a, TH)], query_ps[:, :]).then_inc(query_ready, 1)

            def weight_high(e):
                act.wait_ge(w_scaled, e + 1)
                act.copy(w_hi_flat[:, bass.ts(e, 3 * D)], w_f32_flat[:, bass.ts(e, 3 * D)]).then_inc(w_hi_ready, 1)

            def evac_attnT(a):
                act.wait_ge(attnT_in_ps, a + 1)
                if is_first(a):
                    act.wait_ge(consts_ready, 4)
                else:
                    act.wait_ge(proj_in_ps, a)
                act.copy(attnT[0:V, :], bank_a[0:V, :]).then_inc(attnT_ready, 1)

            def hT_high(a):
                act.wait_ge(hT_in_ps, a + 1)
                act.copy(hT_hi[:, bass.ts(a, TH)], bank_a[:, :]).then_inc(hT_hi_ready, 1)

            def silu_unit(g, k, c):
                u = C * (NE * g + k) + c
                b = (C * k + c) % UBUF
                act.wait_ge(gate_in_ps, u + 1)
                if not isinstance(u, int) or u >= UBUF:
                    act.wait_ge(hid_ready, u - UBUF + 1)
                act.activation(silu[:, b, :], gate_ps[c][:, :], ACT.Silu,
                               scale=1.0 / (ACT_SCALE * W_SCALE)).then_inc(silu_ready, 1)

            def hid_high(g, k, c):
                s = NE * g + k
                u = C * s + c
                act.wait_ge(hid_ready, u + 1)
                act.wait_ge(y_in_ps, 1 + NE * g + max(k - NBUF + 1, 0))
                act.copy(hid_hi[:, k % NBUF, c, :], hid[:, (C * k + c) % UBUF, :]).then_inc(hid_hi_ready, 1)

            evac_qT(0)
            evac_cT(0)

            def scores_body(a, last=False):
                softmax_exp(a)
                if not last:
                    evac_qT(a + 1)
                    evac_cT(a + 1)
                evac_query(a)
                weight_high(a)

            with act.Fori(0, G - 1) as a:
                scores_body(a)
            scores_body(G - 1, last=True)
            weight_high(NE - 1)
            evac_attnT(0)
            hT_high(0)
            silu_unit(0, 0, 0)
            silu_unit(0, 0, 1)
            hid_high(0, 0, 0)
            silu_unit(0, 1, 0)
            hid_high(0, 0, 1)
            silu_unit(0, 1, 1)
            hid_high(0, 1, 0)

            def body(g, last=False):
                for k in range(LAG, NE if last else NE + LAG):
                    silu_unit(g, k, 0)
                    hid_high(g, k - 1, 1)
                    if not last:
                        if k == 3:
                            evac_attnT(g + 1)
                        if k == 8:
                            hT_high(g + 1)
                    silu_unit(g, k, 1)
                    hid_high(g, k, 0)
                if last:
                    hid_high(g, NE - 1, 1)

            with act.Fori(0, G - 1) as g:
                body(g)
            body(G - 1, last=True)

        @block.vector
        def _(dve):
            chain = {"base": 0, "n": 0}

            def link(ins):
                chain["n"] += 1
                ins.then_inc(dve_step, 1)
                dve.wait_ge(dve_step, chain["base"] + chain["n"])

            def norm_stats(src, n, mean, var, scale=1.0):
                for t in range(n):
                    ins = dve.bn_stats(stats[:, t, :], src(t))
                link(ins)
                m_even, m_odd = stats[:, 0:n, 1], stats[:, 0:n, 4]
                m2, diff, sq = mean2[:, 0:n], half_diff[:, 0:n], sq_sum[:, 0:n]
                dve.tensor_tensor(m2, m_even, m_odd, ALU.add)
                dve.tensor_tensor(diff, m_even, m_odd, ALU.subtract)
                link(dve.tensor_tensor(sq, stats[:, 0:n, 2], stats[:, 0:n, 5], ALU.add))
                dve.tensor_scalar(mean, m2, 0.5, None, ALU.mult)
                link(dve.tensor_tensor(diff, diff, diff, ALU.mult))
                link(dve.scalar_tensor_tensor(out=sq, in0=diff, scalar=H / 4, in1=sq,
                                              op0=ALU.mult, op1=ALU.add))
                dve.tensor_scalar(var, sq, 1.0 / (H * scale * scale),
                                  LN_EPS / (scale * scale), ALU.mult, ALU.add).then_inc(var_ready, 1)

            def normalise(dst, src, mean, rstd):
                for t in range(T):
                    ins = dve.tensor_scalar(dst[:, tile_cols(t)], src(t), mean(t), rstd(t),
                                            ALU.subtract, ALU.mult)
                return ins

            def x_tile(a):
                return lambda t: x_all[:, bass.ds(a * TH + t * H, H)]

            def column(v, a=0):
                return lambda t: v[:, bass.ds(a * T + t, 1)]

            def norm_x(a):
                if not is_first(a):
                    dve.wait_ge(xT_in_ps, a)
                normalise(xn, x_tile(a), column(mean_x, a), column(rstd_x, a)).then_inc(xn_ready, 1)

            def row_max(a):
                dve.wait_ge(score_in_ps, a + 1)
                if not is_first(a):
                    dve.wait_ge(exp_ready, a)
                dve.tensor_reduce(neg_max[:, :], score_ps[:, 0:TV].rearrange("p (t v) -> p t v", v=V),
                                  AX.X, ALU.max, negate=True).then_inc(max_ready, 1)

            def evac_ctxW(a):
                dve.wait_ge(ctxW_in_ps, a + 1)
                dve.tensor_copy(ctxW[0:V, bass.ts(a, TH)], ctxW_ps[0:V, :]).then_inc(ctxW_ready, 1)

            def attn_div(a):
                if not is_first(a):
                    dve.wait_ge(attnT_in_ps, a)
                link(dve.reciprocal(attn_rec[:, :], expd_sum[:, bass.ts(a, T)]))
                for t in range(T):
                    ins = dve.tensor_scalar(attn[:, t, :], expd[:, bass.ds(a * TV + t * V, V)],
                                            attn_rec[:, t:t + 1], None, ALU.mult)
                ins.then_inc(attn_ready, 1)

            def proj_tile(t):
                return proj[:, tile_cols(t)]

            def x1_tile(t):
                return x1[:, tile_cols(t)]

            def stats_proj(a):
                dve.wait_ge(proj_in_ps, a + 1)
                link(dve.tensor_tensor(proj[:, :], bank_b[:, :], query_W[:, bass.ts(a, TH)], ALU.add))
                norm_stats(proj_tile, T, mean[:, :], var_eps[:, :])

            def norm_proj(a):
                dve.wait_ge(rstd_ready, norm_count(a, 0))
                normalise(pn, proj_tile, column(mean), column(rstd)).then_inc(pn_ready, 1)

            def stats_x1(a):
                dve.wait_ge(x1_ready, a + 1)
                norm_stats(x1_tile, T, mean[:, :], var_eps[:, :], ACT_SCALE)

            def norm_x1(a):
                dve.wait_ge(rstd_ready, norm_count(a, 1))
                if not (isinstance(a, int) and a == 0):
                    dve.wait_ge(hT_in_ps, a)
                normalise(hn, x1_tile, column(mean), column(rstd)).then_inc(hn_ready, 1)

            def hT_low(a):
                dve.wait_ge(hT_hi_ready, a + 1)
                cols = bass.ts(a, TH)
                dve.tensor_tensor(hT_lo[:, cols], bank_a[:, :], hT_hi[:, cols],
                                  ALU.subtract).then_inc(hT_lo_ready, 1)

            def over(v):
                return v[:, :].unsqueeze(2).to_broadcast([P, T, E])

            def route_pick_first(a):
                dve.wait_ge(logit_in_ps, a + 1)
                dve.tensor_scalar(logit[:, :, :], bank_b[:, 0:T * E].rearrange("p (t e) -> p t e", e=E),
                                  1.0 / (ACT_SCALE * W_SCALE), None, ALU.mult).then_inc(logit_read, 1)
                dve.wait_ge(logit_read, a + 1)
                link(dve.tensor_reduce(top[:, :], logit[:, :, :], AX.X, ALU.max))
                dve.tensor_tensor(below_top[:, :, :], logit[:, :, :], over(top),
                                  ALU.subtract).then_inc(below_ready, 1)
                link(dve.tensor_tensor(code[:, :, :], logit[:, :, :], over(top), ALU.is_ge))
                link(dve.tensor_tensor(code[:, :, :], code[:, :, :], first_code[:, :, :], ALU.mult))
                link(dve.tensor_reduce(best[:, :], code[:, :, :], AX.X, ALU.max))
                link(dve.tensor_tensor(one1[:, :, :], first_code[:, :, :], over(best), ALU.is_equal))

            def route_pick_second():
                link(dve.scalar_tensor_tensor(out=logit2[:, :, :], in0=one1[:, :, :], scalar=-1e30,
                                              in1=logit[:, :, :], op0=ALU.mult, op1=ALU.add))
                link(dve.tensor_reduce(top[:, :], logit2[:, :, :], AX.X, ALU.max))
                link(dve.tensor_tensor(code[:, :, :], logit2[:, :, :], over(top), ALU.is_ge))
                link(dve.tensor_tensor(code[:, :, :], code[:, :, :], first_code[:, :, :], ALU.mult))
                link(dve.tensor_reduce(best[:, :], code[:, :, :], AX.X, ALU.max))
                link(dve.tensor_tensor(one2[:, :, :], first_code[:, :, :], over(best), ALU.is_equal))
                link(dve.tensor_tensor(picked[:, :, :], one1[:, :, :], one2[:, :, :], ALU.add))

            def route_weights(a):
                dve.wait_ge(expo_ready, a + 1)
                dve.tensor_reduce(sum_all[:, :], expo[:, :, :], AX.X, ALU.add)
                link(dve.tensor_tensor(chosen[:, :, :], expo[:, :, :], picked[:, :, :], ALU.mult))
                link(dve.tensor_reduce(sum_two[:, :], chosen[:, :, :], AX.X, ALU.add))
                link(dve.scalar_tensor_tensor(out=sum_two[:, :], in0=sum_all[:, :], scalar=TOPK_EPS,
                                              in1=sum_two[:, :], op0=ALU.mult, op1=ALU.add))
                link(dve.reciprocal(sum_two[:, :], sum_two[:, :]))
                link(dve.tensor_scalar(sum_two[:, :], sum_two[:, :], ffn_gain[:, 0:1], None, ALU.mult))
                link(dve.tensor_tensor(weight[:, :, :], chosen[:, :, :], over(sum_two), ALU.mult))

            def hid_unit(g, k, c):
                u = C * (NE * g + k) + c
                b = (C * k + c) % UBUF
                dve.wait_ge(up_in_ps, u + 1)
                dve.wait_ge(silu_ready, u + 1)
                if not isinstance(u, int) or u >= UBUF:
                    dve.wait_ge(hid_lo_ready, u - UBUF + 1)
                dve.scalar_tensor_tensor(out=hid[:, b, :], in0=up_ps[c][:, :],
                                         scalar=HID_SCALE / (ACT_SCALE * W_SCALE), in1=silu[:, b, :],
                                         op0=ALU.mult, op1=ALU.mult).then_inc(hid_ready, 1)

            def add_y(g, k):
                s = NE * g + k
                dve.wait_ge(y_in_ps, 1 + s + 1)
                dve.wait_ge(y_added, 1 + s)
                if k == 0:
                    ins = dve.scalar_tensor_tensor(out=x_all[:, bass.ts(g, TH)], in0=y_ps[0][:, :],
                                                   scalar=ffn_gain[:, 0:1], in1=x1[:, :], op0=ALU.mult, op1=ALU.add)
                else:
                    for t in range(T):
                        xt = x_tile(g)(t)
                        ins = dve.scalar_tensor_tensor(out=xt, in0=y_ps[k % 2][:, tile_cols(t)],
                                                       scalar=weight[:, t, k - 1:k], in1=xt,
                                                       op0=ALU.mult, op1=ALU.add)
                ins.then_inc(y_added, 1)

            def stats_x(n):
                lo, hi = x_parts[n]
                dve.wait_ge(x_in[n], 16)
                norm_stats(x_tile(lo // T), hi - lo, mean_x[:, lo:hi], var_x[:, lo:hi])

            stats_x(0)
            dve.wait_ge(y_in_ps, 1)
            dve.tensor_copy(w_ctx_T[:, :], w_T_ps[:, 0:H])
            dve.tensor_copy(w_qry_T[:, :], w_T_ps[:, H:2 * H]).then_inc(y_added, 1)
            dve.wait_ge(rstd_ready, 1)
            norm_x(0)
            stats_x(1)
            dve.wait_ge(rstd_ready, 2)
            norm_x(1)
            row_max(0)
            evac_ctxW(0)
            dve.wait_ge(tanh_ready, 1)
            dve.tensor_scalar(gain[:, :], gain[:, :], g_tanh[:, 0:1], None, ALU.mult).then_inc(gain_ready, 1)
            dve.tensor_scalar(shift[:, :], shift[:, :], g_tanh[:, 0:1], None, ALU.mult).then_inc(gain_ready, 1)
            link(dve.tensor_scalar(ffn_gain[:, :], g_tanh[:, 1:2], 1.0 / (HID_SCALE * W_SCALE), None, ALU.mult))
            dve.wait_ge(gw_hi_ready, 1)
            dve.scalar_tensor_tensor(out=gw_lo[:, :], in0=gw_f32[:, :], scalar=W_SCALE, in1=gw_hi[:, :],
                                     op0=ALU.mult, op1=ALU.subtract).then_inc(gw_ready, 1)
            stats_x(2)
            norm_x(2)
            dve.wait_ge(rstd_ready, 3)
            with dve.Fori(1, G - 2) as a:
                row_max(a)
                norm_x(a + 2)
                evac_ctxW(a)
            for a in (G - 2, G - 1):
                row_max(a)
                evac_ctxW(a)
            dve.wait_ge(exp_ready, G)
            dve.wait_ge(query_ready, G)
            attn_div(0)
            stats_proj(0)
            norm_proj(0)
            stats_x1(0)
            norm_x1(0)
            hT_low(0)
            route_pick_first(0)
            route_pick_second()
            for k in range(LAG):
                for c in range(C):
                    hid_unit(0, k, c)

            def body(g, last=False):
                for k in range(LAG, NE + LAG):
                    if k < NE or not last:
                        hid_unit(g, k, 0)
                    if not last:
                        if k == 2:
                            attn_div(g + 1)
                        if k == 7:
                            norm_x1(g + 1)
                        if k == 8:
                            hT_low(g + 1)
                        if k == 10:
                            route_pick_second()
                    if k == 3:
                        route_weights(g)
                    if k < NE or not last:
                        hid_unit(g, k, 1)
                    if not last:
                        if k == 4:
                            stats_proj(g + 1)
                        if k == 5:
                            norm_proj(g + 1)
                        if k == 6:
                            stats_x1(g + 1)
                        if k == 9:
                            route_pick_first(g + 1)
                    add_y(g, k - LAG)

            before = chain["n"]
            per_body = 28
            with dve.Fori(0, G - 1) as g:
                chain["base"], chain["n"] = before + g * per_body, 0
                body(g)
                assert chain["n"] == per_body, chain["n"]
            chain["base"], chain["n"] = before + (G - 1) * per_body, 0
            body(G - 1, last=True)

        @block.tensor
        def _(pe):
            def transpose_in(a):
                pe.wait_ge(xn_ready, a + 1)
                if not is_first(a):
                    pe.wait_ge(qT_ready, a)
                for t in range(T):
                    ins = pe.transpose(bank_a[:, tile_cols(t)], xn[:, tile_cols(t)], ident[:, :])
                ins.then_inc(xT_in_ps, 1)
                pe.wait_ge(ctx_landed, 16 * (a + 1))
                if not is_first(a):
                    pe.wait_ge(cT_ready, a)
                for t in range(T):
                    ins = pe.transpose(bank_b[:, tile_cols(t, V)], ctx_in[:, t, :], ident[0:V, 0:V])
                ins.then_inc(ctxT_in_ps, 1)

            def scores(a):
                pe.wait_ge(qT_ready, a + 1)
                pe.wait_ge(cT_ready, a + 1)
                if not is_first(a):
                    pe.wait_ge(exp_ready, a)
                for t in range(T):
                    ins = pe.matmul(score_ps[:, tile_cols(t, V)], qT[:, tile_cols(t)], cT[:, tile_cols(t, V)],
                                    start=True, stop=True)
                ins.then_inc(score_in_ps, 1)
                if not is_first(a):
                    pe.wait_ge(query_ready, a)
                for t in range(T):
                    ins = pe.matmul(query_ps[:, tile_cols(t)], qT[:, tile_cols(t)], w_qry_T[:, :],
                                    start=True, stop=True)
                ins.then_inc(query_in_ps, 1)
                if not is_first(a):
                    pe.wait_ge(ctxW_ready, a)
                for t in range(T):
                    ins = pe.matmul(ctxW_ps[0:V, tile_cols(t)], cT[:, tile_cols(t, V)], w_ctx_T[:, :],
                                    start=True, stop=True)
                ins.then_inc(ctxW_in_ps, 1)

            def transpose_attn(a):
                pe.wait_ge(attn_ready, a + 1)
                if not is_first(a):
                    pe.wait_ge(hT_lo_ready, a)
                for t in range(T):
                    ins = pe.transpose(bank_a[0:V, tile_cols(t)], attn[:, t, :], ident[:, :])
                ins.then_inc(attnT_in_ps, 1)

            def project(a):
                pe.wait_ge(attnT_ready, a + 1)
                if not is_first(a):
                    pe.wait_ge(logit_read, a)
                for t in range(T):
                    ins = pe.matmul(bank_b[:, tile_cols(t)], attnT[:, tile_cols(t)],
                                    ctxW[:, bass.ds(a * TH + t * H, H)], start=True, stop=True)
                ins.then_inc(proj_in_ps, 1)

            def transpose_h(a):
                pe.wait_ge(hn_ready, a + 1)
                for t in range(T):
                    ins = pe.transpose(bank_a[:, tile_cols(t)], hn[:, tile_cols(t)], ident[:, :])
                ins.then_inc(hT_in_ps, 1)

            def route_logits(a):
                pe.wait_ge(hT_lo_ready, a + 1)
                for t in range(T):
                    cols = bass.ds(a * TH + t * S, S)
                    o = bank_b[:, tile_cols(t, E)]
                    pe.matmul(o, hT_hi[:, cols], gw_hi[:, :], start=True, stop=False)
                    pe.matmul(o, hT_hi[:, cols], gw_lo[:, :], start=False, stop=False)
                    ins = pe.matmul(o, hT_lo[:, cols], gw_hi[:, :], start=False, stop=True)
                ins.then_inc(logit_in_ps, 1)

            def gate_up(g, k, c):
                s = NE * g + k
                u = C * s + c
                cols = bass.ts(g + k // NE, TH)
                if k == NE and c == 0:
                    pe.wait_ge(hT_lo_ready, g + 2)
                for part, bank, free, done in ((0, gate_ps[c], silu_ready, gate_in_ps),
                                               (1, up_ps[c], hid_ready, up_in_ps)):
                    wh, wl = parts(part, k % NE)
                    if not isinstance(u, int) or u >= C:
                        pe.wait_ge(free, u - 1)
                    pe.matmul(bank[:, :], wh[:, c:D:C], hT_hi[:, cols], start=True, stop=False)
                    pe.matmul(bank[:, :], wh[:, c:D:C], hT_lo[:, cols], start=False, stop=False)
                    pe.matmul(bank[:, :], wl[:, c:D:C], hT_hi[:, cols], start=False,
                              stop=True).then_inc(done, 1)

            def down(g, k):
                s = NE * g + k
                wh, wl = parts(2, k)
                o = y_ps[k % 2]
                pe.wait_ge(hid_lo_ready, C * (s + 1))
                pe.wait_ge(y_added, 1 + (s if k == 0 else s - 1))
                for t in range(T):
                    for c in range(C):
                        hh = hid_hi[:, k % NBUF, c, tile_cols(t)]
                        hl = hid_lo[:, k % NBUF, c, tile_cols(t)]
                        pe.matmul(o[:, tile_cols(t)], hh, wh[:, tile_cols(c, P)], start=(c == 0), stop=False)
                        pe.matmul(o[:, tile_cols(t)], hh, wl[:, tile_cols(c, P)], start=False, stop=False)
                        ins = pe.matmul(o[:, tile_cols(t)], hl, wh[:, tile_cols(c, P)], start=False,
                                        stop=(c == C - 1))
                ins.then_inc(y_in_ps, 1)

            pe.wait_ge(ident_ready, 1)
            pe.wait_ge(small_in, 16 * N_SMALL)
            pe.transpose(w_T_ps[:, 0:H], w_rows[:, 0:H], ident[:, :])
            pe.transpose(w_T_ps[:, H:2 * H], w_rows[:, H:2 * H], ident[:, :]).then_inc(y_in_ps, 1)
            transpose_in(0)
            pe.wait_ge(y_added, 1)
            with pe.Fori(0, G - 1) as a:
                transpose_in(a + 1)
                scores(a)
            scores(G - 1)
            pe.wait_ge(exp_ready, G)
            pe.wait_ge(query_ready, G)
            pe.wait_ge(ctxW_ready, G)
            transpose_attn(0)
            project(0)
            transpose_h(0)
            pe.wait_ge(gw_ready, 1)
            route_logits(0)
            for k in range(LAG):
                pe.wait_ge(w_lo_ready, k + 1)
                for c in range(C):
                    gate_up(0, k, c)
            pe.wait_ge(w_lo_ready, NE)

            def body(g, last=False):
                for k in range(LAG, NE + LAG):
                    if k < NE or not last:
                        gate_up(g, k, 0)
                    if not last:
                        if k == 4:
                            project(g + 1)
                        if k == 9:
                            route_logits(g + 1)
                    if k < NE or not last:
                        gate_up(g, k, 1)
                    if not last:
                        if k == 2:
                            transpose_attn(g + 1)
                        if k == 7:
                            transpose_h(g + 1)
                    down(g, k - LAG)

            with pe.Fori(0, G - 1) as g:
                body(g)
            body(G - 1, last=True)


_INS = ["x", "ctx_1024", "g_xattn", "g_ffn", "L0_xattn_W", "L0_xattn_b", "L0_xattn_gamma", "L0_xattn_beta",
        "L0_ffn_gate_w", "L0_ffn_w_gate", "L0_ffn_w_up", "L0_ffn_w_down", "L0_ffn_ws_gate", "L0_ffn_ws_up",
        "L0_ffn_ws_down"]


def kernel(**inputs):
    import numpy as _np
    import concourse.bacc as _bacc
    from concourse import mybir as _mybir
    from concourse.bass_utils import run_bass_kernel_spmd as _run

    nc = _bacc.Bacc("TRN2", target_bir_lowering=False, num_devices=1)
    arrays, args = {}, []
    for name in _INS:
        a = _np.ascontiguousarray(inputs[name])
        arrays[f"in_{name}"] = a
        args.append(nc.dram_tensor(f"in_{name}", a.shape, _mybir.dt.from_np(a.dtype), kind="ExternalInput").ap())
    shape = inputs["x"].shape
    args.append(nc.dram_tensor("out_0", shape, _mybir.dt.float32, kind="ExternalOutput").ap())
    flamingo_gated_layer(nc, *args)
    r = _run(nc, [arrays], core_ids=[0])
    return r.results[0]["out_0"]
```

```python
from contextlib import ExitStack

import concourse.bass as bass
from concourse import mybir

ALU = mybir.AluOpType
ACT = mybir.ActivationFunctionType
AX = mybir.AxisListType
F32 = mybir.dt.float32
F16 = mybir.dt.float16

P = 128
LN_EPS = 1e-5
TOPK_EPS = 1e-20
ACT_SCALE = 64.0
W_SCALE = 64.0
HID_SCALE = 4.0


def flamingo_gated_layer(nc, x, ctx_kv, g_xattn, g_ffn, W, b, gamma, beta,
                         gate_w, w_gate, w_up, w_down, ws_gate, ws_up, ws_down, out):
    B, S, H = x.shape
    V = ctx_kv.shape[1]
    E, _, D = w_gate.shape
    assert S == P and H == P and D == 2 * P
    T = 4
    G = B // T
    TH = T * H
    TV = T * V
    NE = E + 1
    C = D // P
    UNITS = C * NE
    NBUF = 3
    UBUF = 3
    HBUF = 6
    LAG = 2
    SQUARE_SCALE = (H * ACT_SCALE ** 2) ** -0.5
    assert NE % NBUF == 0 and UNITS % UBUF == 0 and UNITS % HBUF == 0

    with ExitStack() as stack:
        def sb(name, shape, dt=F32):
            return stack.enter_context(nc.sbuf_tensor(name, shape, dt))

        def ps(name, shape):
            return stack.enter_context(nc.psum_tensor(name, shape, F32))

        def sem(name):
            return stack.enter_context(nc.semaphore(name))

        ident = sb("ident", [P, P])
        w_rows = sb("w_rows", [P, 2 * H])
        w_ctx_T = sb("w_ctx_T", [P, H])
        w_qry_T = sb("w_qry_T", [P, H])
        gain = sb("gain", [P, TH])
        shift = sb("shift", [P, TH])
        g_raw = sb("g_raw", [P, 2])
        g_tanh = sb("g_tanh", [P, 2])
        ffn_gain = sb("ffn_gain", [P, 1])
        first_code = sb("first_code", [P, T, E])
        w_f32 = sb("w_f32", [P, NE, 3, D])
        w_hi = sb("w_hi", [P, NE, 3, D], F16)
        w_lo = sb("w_lo", [P, NE, 3, D], F16)
        gw_f32 = sb("gw_f32", [P, E])
        gw_hi = sb("gw_hi", [P, E], F16)
        gw_lo = sb("gw_lo", [P, E], F16)
        x_all = sb("x_all", [P, B * H])
        expd = sb("expd", [P, B * V])
        expd_sum = sb("expd_sum", [P, B])
        query_W = sb("query_W", [P, B * H])
        ctxW = sb("ctxW", [V + 1, B * H])
        hT_hi = sb("hT_hi", [P, B * S], F16)
        hT_lo = sb("hT_lo", [P, B * S], F16)
        stats = sb("stats", [P, T, 6])
        mean2 = sb("mean2", [P, T])
        mean = sb("mean", [P, T])
        sum_h = sb("sum_h", [P, T])
        neg_mean_h = sb("neg_mean_h", [P, T])
        neg_mean_sq = sb("neg_mean_sq", [P, T])
        mean_square_h = sb("mean_square_h", [P, T])
        scaled_eps = sb("scaled_eps", [P, T])
        mean_x = sb("mean_x", [P, 2, T])
        half_diff = sb("half_diff", [P, T])
        sq_sum = sb("sq_sum", [P, T])
        var_x = sb("var_x", [P, 2, T])
        rstd_x = sb("rstd_x", [P, 2, T])
        var_eps = sb("var_eps", [P, T])
        var_eps_h = sb("var_eps_h", [P, T])
        rstd = sb("rstd", [P, T])
        rstd_h = sb("rstd_h", [P, T])
        bias_h = sb("bias_h", [P, T])
        minus_half = sb("minus_half", [P, T])
        ctx_in = sb("ctx_in", [V, 2, T, H])
        xn = sb("xn", [P, 2, TH])
        qT = sb("qT", [P, 2, TH])
        cT = sb("cT", [P, 2, TV])
        neg_max = sb("neg_max", [P, T])
        attn = sb("attn", [P, T, V])
        attn_rec = sb("attn_rec", [P, B])
        attnT = sb("attnT", [V + 1, TH])
        proj = sb("proj", [P, TH])
        xs = sb("xs", [P, TH])
        x1 = sb("x1", [P, TH])
        hn = sb("hn", [P, TH])
        logit = sb("logit", [P, T, E])
        top = sb("top", [P, T])
        code = sb("code", [P, T, E])
        best = sb("best", [P, T])
        one1 = sb("one1", [P, T, E])
        logit2 = sb("logit2", [P, T, E])
        one2 = sb("one2", [P, T, E])
        picked = sb("picked", [P, T, E])
        below_top = sb("below_top", [P, T, E])
        euler = sb("euler", [P, E])
        expo = sb("expo", [P, T, E])
        chosen = sb("chosen", [P, T, E])
        sum_all = sb("sum_all", [P, T])
        sum_two = sb("sum_two", [P, T])
        weight = sb("weight", [P, T, E])
        silu = sb("silu", [P, UBUF, TH])
        hid = sb("hid", [P, HBUF, TH])
        hid_hi = sb("hid_hi", [P, NBUF, C, TH], F16)
        hid_lo = sb("hid_lo", [P, NBUF, C, TH], F16)

        gate_ps = [ps(f"gate_ps{c}", [P, TH]) for c in range(C)]
        up_ps = [ps(f"up_ps{c}", [P, TH]) for c in range(C)]
        y_ps = [ps(f"y_ps{i}", [P, TH]) for i in range(2)]
        bank_a = ps("bank_a", [P, 512])
        bank_b = ps("bank_b", [P, 512])
        attn_bank = [gate_ps[1], bank_a]
        proj_bank = [up_ps[1], bank_b]
        score_ps, ctxW_ps, query_ps, w_T_ps = y_ps[0], y_ps[1], gate_ps[0], up_ps[0]

        x_parts = [(0, T), (T, 2 * T), (2 * T, 4 * T), (4 * T, B)]
        x_in = [sem(f"x_in{i}") for i in range(len(x_parts))]
        ctx_landed = [sem(f"ctx_landed{i}") for i in range(2)]
        w_rows_in = sem("w_rows_in")
        small_in = sem("small_in")
        N_SMALL = 6
        w_chunks = [(0, 1), (1, 4), (4, 6), (6, NE)]
        DVE_LOW = 6
        w_in = [sem(f"w_in{i}") for i in range(len(w_chunks))]
        ident_ready = sem("ident_ready")
        consts_ready = sem("consts_ready")
        tanh_ready = sem("tanh_ready")
        gain_ready = sem("gain_ready")
        w_scaled = sem("w_scaled")
        w_hi_pool = sem("w_hi_pool")
        w_hi_act = sem("w_hi_act")
        w_lo_dve = sem("w_lo_dve")
        w_lo_pool = sem("w_lo_pool")
        gw_hi_ready = sem("gw_hi_ready")
        gw_ready = sem("gw_ready")
        dve_step = sem("dve_step")
        pool_step = sem("pool_step")
        var_ready = sem("var_ready")
        rstd_ready = sem("rstd_ready")
        xn_ready = sem("xn_ready")
        xT_in_ps = sem("xT_in_ps")
        ctxT_in_ps = sem("ctxT_in_ps")
        qT_ready = sem("qT_ready")
        cT_ready = sem("cT_ready")
        score_in_ps = sem("score_in_ps")
        query_in_ps = sem("query_in_ps")
        ctxW_in_ps = sem("ctxW_in_ps")
        max_ready = sem("max_ready")
        exp_ready = sem("exp_ready")
        query_ready = sem("query_ready")
        ctxW_ready = sem("ctxW_ready")
        rec_ready = sem("rec_ready")
        attn_ready = sem("attn_ready")
        attnT_in_ps = sem("attnT_in_ps")
        attnT_ready = sem("attnT_ready")
        proj_in_ps = sem("proj_in_ps")
        xs_ready = sem("xs_ready")
        x1_ready = sem("x1_ready")
        neg_mean_h_ready = sem("neg_mean_h_ready")
        mean_square_h_ready = sem("mean_square_h_ready")
        var_h_ready = sem("var_h_ready")
        rstd_h_ready = sem("rstd_h_ready")
        bias_h_ready = sem("bias_h_ready")
        hn_ready = sem("hn_ready")
        hT_in_ps = sem("hT_in_ps")
        hT_hi_ready = sem("hT_hi_ready")
        hT_lo_ready = sem("hT_lo_ready")
        logit_in_ps = sem("logit_in_ps")
        logit_read = sem("logit_read")
        below_ready = sem("below_ready")
        expo_ready = sem("expo_ready")
        gate_in_ps = sem("gate_in_ps")
        up_in_ps = sem("up_in_ps")
        silu_ready = sem("silu_ready")
        hid_ready = sem("hid_ready")
        hid_hi_ready = sem("hid_hi_ready")
        hid_lo_ready = sem("hid_lo_ready")
        y_in_ps = sem("y_in_ps")
        y_added = sem("y_added")
        stored = sem("stored")

        x_d = x.rearrange("b p h -> p b h")
        out_d = out.rearrange("b p h -> p b h")
        ctx_d = ctx_kv.rearrange("b v h -> v b h")
        w_f32_flat = w_f32[:, :, :, :].rearrange("p e a d -> p (e a d)")
        w_hi_flat = w_hi[:, :, :, :].rearrange("p e a d -> p (e a d)")
        N_PAIRS = 2
        PAIRS_END = 1 + 2 * N_PAIRS
        assert G == PAIRS_END + 3
        x_v = x_all[:, :].rearrange("p (b h) -> p b h", h=H)

        block = stack.enter_context(nc.Block())

        def norm_count(a):
            return G + a + 1

        def is_first(a):
            return isinstance(a, int) and a == 0

        def tile_cols(t, n=H):
            return slice(t * n, (t + 1) * n)

        def parts(t, e):
            return w_hi[:, e, t, :], w_lo[:, e, t, :]

        @block.sync
        def _(sp):
            def load_x(n):
                lo, hi = x_parts[n]
                sp.dma_start(x_v[:, lo:hi, :], x_d[:, lo:hi, :]).then_inc(x_in[n], 16)

            def load_weights(n):
                lo, hi = w_chunks[n]
                if lo == 0:
                    loads = ((0, ws_gate), (1, ws_up), (2, ws_down.rearrange("(p c) h -> p (c h)", c=C)))
                    for part, src in loads:
                        sp.dma_start(w_f32[:, 0, part, :], src).then_inc(w_in[n], 16)
                    return
                loads = ((0, w_gate, "e h d -> h e d"), (1, w_up, "e h d -> h e d"),
                         (2, w_down, "e (p c) h -> p e (c h)"))
                for part, src, order in loads:
                    sizes = {"c": C} if part == 2 else {}
                    sp.dma_start(w_f32[:, lo:hi, part, :],
                                 src[lo - 1:hi - 1].rearrange(order, **sizes)).then_inc(w_in[n], 16)

            def load_ctx(a, buf):
                sp.dma_start(ctx_in[:, buf, :, :], ctx_d[:, bass.ds(a * T, T), :]).then_inc(ctx_landed[buf], 16)

            load_x(0)
            load_ctx(0, 0)
            load_x(1)
            load_ctx(1, 1)
            load_x(2)
            load_x(3)
            load_weights(0)
            load_weights(1)
            with sp.Fori(0, G // 2 - 1) as pair:
                for buf in range(2):
                    sp.wait_ge(ctxT_in_ps, 2 * pair + buf + 1)
                    load_ctx(2 * pair + 2 + buf, buf)
            load_weights(2)
            load_weights(3)

            def store(g):
                sp.wait_ge(y_added, 1 + NE * (g + 1))
                sp.dma_start(out_d[:, bass.ts(g, T), :], x_v[:, bass.ts(g, T), :]).then_inc(stored, 16)

            with sp.Fori(0, G) as g:
                store(g)
            sp.wait_ge(stored, 16 * G)

        @block.gpsimd
        def _(pool):
            pool.memset(ident[:, :], 0.0).then_inc(pool_step, 1)
            pool.memset(minus_half[:, :], -0.5).then_inc(consts_ready, 1)
            pool.wait_ge(pool_step, 1)
            pool.affine_select(out=ident[:, :], in_=ident[:, :], compare_op=ALU.not_equal, fill=1.0,
                               base=0, pattern=[[-1, P]], channel_multiplier=1).then_inc(ident_ready, 1)
            pool.wait_ge(consts_ready, 1)

            def power(dst, src, n, count):
                pool.wait_ge(var_ready, count)
                pool.tensor_tensor(dst, src, minus_half[:, 0:n], ALU.pow).then_inc(rstd_ready, 1)

            def rstd_proj(a):
                power(rstd[:, :], var_eps[:, :], T, norm_count(a))

            def rstd_x1(a):
                pool.wait_ge(mean_square_h_ready, a + 1)
                pool.tensor_tensor(var_eps_h[:, :], mean_square_h[:, :], scaled_eps[:, :],
                                   ALU.add).then_inc(var_h_ready, 1)
                pool.wait_ge(var_h_ready, a + 1)
                pool.tensor_tensor(rstd_h[:, :], var_eps_h[:, :], minus_half[:, :], ALU.pow).then_inc(rstd_h_ready, 1)
                pool.wait_ge(rstd_h_ready, a + 1)
                pool.tensor_tensor(bias_h[:, :], neg_mean_h[:, :], rstd_h[:, :], ALU.mult).then_inc(bias_h_ready, 1)

            def shifted(a):
                if not is_first(a):
                    pool.wait_ge(x1_ready, a)
                pool.tensor_tensor(xs[:, :], x_all[:, bass.ts(a, TH)], shift[:, :], ALU.add).then_inc(xs_ready, 1)

            def route_exp(a, t):
                pool.wait_ge(below_ready, a + 1)
                pool.tensor_tensor(expo[:, t, :], euler[:, :], below_top[:, t, :], ALU.pow).then_inc(expo_ready, 1)

            def hid_low(g, k, c):
                s = NE * g + k
                u = C * s + c
                pool.wait_ge(hid_hi_ready, u + 1)
                pool.tensor_tensor(hid_lo[:, k % NBUF, c, :], hid[:, (C * k + c) % HBUF, :],
                                   hid_hi[:, k % NBUF, c, :], ALU.subtract).then_inc(hid_lo_ready, 1)

            def rstd_x_pow(a):
                power(rstd_x[:, a % 2, :], var_x[:, a % 2, :], T, a + 1)

            def weight_high(e):
                pool.tensor_scalar(w_hi[:, e, :, :].rearrange("p a d -> p (a d)"),
                                   w_f32[:, e, :, :].rearrange("p a d -> p (a d)"),
                                   W_SCALE, 1.0, ALU.mult, ALU.mult).then_inc(w_hi_pool, 1)

            def weight_low(e):
                pool.wait_ge(w_hi_act, e - DVE_LOW + 1)
                flat = w_f32[:, e, :, :].rearrange("p a d -> p (a d)")
                pool.tensor_scalar(flat, flat, W_SCALE, 1.0, ALU.mult, ALU.mult).then_inc(w_scaled, 1)
                pool.wait_ge(w_scaled, e - DVE_LOW + 1)
                pool.tensor_tensor(w_lo[:, e, :, :].rearrange("p a d -> p (a d)"), flat,
                                   w_hi[:, e, :, :].rearrange("p a d -> p (a d)"),
                                   ALU.subtract).then_inc(w_lo_pool, 1)

            rstd_x_pow(0)
            rstd_x_pow(1)
            pool.memset(attnT[:, :], 1.0).then_inc(consts_ready, 1)
            pool.memset(scaled_eps[:, :], LN_EPS / ACT_SCALE ** 2).then_inc(consts_ready, 1)
            for e in range(E):
                last = pool.memset(first_code[:, :, e:e + 1], float(E - e))
            last.then_inc(consts_ready, 1)
            pool.memset(euler[:, :], 2.718281828459045).then_inc(consts_ready, 1)
            rstd_x_pow(2)
            rstd_x_pow(3)
            pool.wait_ge(w_in[0], 48)
            weight_high(0)
            rstd_x_pow(4)
            pool.wait_ge(w_in[1], 48)
            for e in range(1, 4):
                weight_high(e)
                rstd_x_pow(4 + e)
            pool.wait_ge(w_in[2], 48)
            for e in range(4, DVE_LOW):
                weight_high(e)
            pool.wait_ge(consts_ready, 5)
            pool.wait_ge(gain_ready, 2)
            shifted(0)
            rstd_proj(0)
            weight_low(DVE_LOW)
            rstd_x1(0)
            for e in range(DVE_LOW + 1, NE):
                weight_low(e)
            hid_low(0, 0, 0)
            route_exp(0, 0)
            hid_low(0, 0, 1)
            route_exp(0, 1)
            hid_low(0, 1, 0)
            route_exp(0, 2)

            def body(g, last=False):
                for k in range(LAG, NE if last else NE + LAG):
                    if not last and k == 6:
                        rstd_x1(g + 1)
                    hid_low(g, k - 1, 1)
                    if k == 2:
                        route_exp(g, 3)
                    if not last:
                        if k == 10:
                            route_exp(g + 1, 1)
                    hid_low(g, k, 0)
                    if not last:
                        if k == 3:
                            shifted(g + 1)
                        if k == 4:
                            rstd_proj(g + 1)
                        if k == 9:
                            route_exp(g + 1, 0)
                        if k == 10:
                            route_exp(g + 1, 2)
                if last:
                    hid_low(g, NE - 1, 1)

            with pool.Fori(0, G - 1) as g:
                body(g)
            body(G - 1, last=True)

        @block.scalar
        def _(act):
            act.dma_start(w_rows[:, :], W).then_inc(w_rows_in, 16)
            act.dma_start(g_raw[:, 0:1], g_xattn.partition_broadcast(P)).then_inc(small_in, 16)
            act.dma_start(g_raw[:, 1:2], g_ffn.partition_broadcast(P)).then_inc(small_in, 16)
            act.dma_start(gw_f32[:, :], gate_w).then_inc(small_in, 16)
            for dst, src in ((gain, gamma), (shift, beta)):
                act.dma_start(dst[:, :].rearrange("p (t h) -> p t h", h=H),
                              src.unsqueeze(0).unsqueeze(0).to_broadcast([P, T, H])).then_inc(small_in, 16)
            act.dma_start(ctxW[V:V + 1, :].rearrange("o (b h) -> o b h", h=H),
                          b.unsqueeze(0).unsqueeze(0).to_broadcast([1, B, H])).then_inc(small_in, 16)
            def evac_qT(a, buf):
                act.wait_ge(xT_in_ps, a + 1)
                if not (isinstance(a, int) and a < 2):
                    act.wait_ge(query_in_ps, a - 1)
                act.copy(qT[:, buf, :], bank_a[:, :]).then_inc(qT_ready, 1)

            def evac_cT(a, buf):
                act.wait_ge(ctxT_in_ps, a + 1)
                if not (isinstance(a, int) and a < 2):
                    act.wait_ge(ctxW_in_ps, a - 1)
                act.copy(cT[:, buf, :], bank_b[:, 0:TV]).then_inc(cT_ready, 1)

            def softmax_exp(a):
                act.wait_ge(max_ready, a + 1)
                for t in range(T):
                    ins = act.activation(expd[:, bass.ds(a * TV + t * V, V)], score_ps[:, tile_cols(t, V)],
                                         ACT.Exp, bias=neg_max[:, t:t + 1],
                                         accum_out=expd_sum[:, bass.ds(a * T + t, 1)])
                ins.then_inc(exp_ready, 1)

            def evac_query(a):
                act.wait_ge(query_in_ps, a + 1)
                act.copy(query_W[:, bass.ts(a, TH)], query_ps[:, :]).then_inc(query_ready, 1)

            def weight_high(e):
                act.mul(w_hi_flat[:, bass.ts(e, 3 * D)], w_f32_flat[:, bass.ts(e, 3 * D)],
                        W_SCALE).then_inc(w_hi_act, 1)

            def evac_ctxW(a):
                act.wait_ge(ctxW_in_ps, a + 1)
                act.copy(ctxW[0:V, bass.ts(a, TH)], ctxW_ps[0:V, :]).then_inc(ctxW_ready, 1)

            def attn_div(a):
                if is_first(a):
                    act.wait_ge(rec_ready, 1)
                else:
                    act.wait_ge(attnT_in_ps, a)
                for t in range(T):
                    ins = act.mul(attn[:, t, :], expd[:, bass.ds(a * TV + t * V, V)],
                                  attn_rec[:, bass.ds(a * T + t, 1)])
                ins.then_inc(attn_ready, 1)

            def evac_attnT(a):
                act.wait_ge(attnT_in_ps, a + 1)
                if is_first(a):
                    act.wait_ge(consts_ready, 5)
                else:
                    act.wait_ge(proj_in_ps, a)
                act.copy(attnT[0:V, :], attn_bank[not is_first(a)][0:V, :]).then_inc(attnT_ready, 1)

            def squares_x1(a):
                act.wait_ge(neg_mean_h_ready, a + 1)
                if not is_first(a):
                    act.wait_ge(hT_in_ps, a)
                for t in range(T):
                    ins = act.activation(hn[:, tile_cols(t)], x1[:, tile_cols(t)], ACT.Square,
                                         scale=SQUARE_SCALE, bias=neg_mean_sq[:, t:t + 1], accum_out=mean_square_h[:, t:t + 1])
                ins.then_inc(mean_square_h_ready, 1)

            def norm_x1(a, half):
                act.wait_ge(bias_h_ready, a + 1)
                for t in range(half * T // 2, (half + 1) * T // 2):
                    ins = act.activation(hn[:, tile_cols(t)], x1[:, tile_cols(t)], ACT.Identity,
                                         scale=rstd_h[:, t:t + 1], bias=bias_h[:, t:t + 1])
                ins.then_inc(hn_ready, 1)

            def hT_high(a):
                act.wait_ge(hT_in_ps, a + 1)
                act.copy(hT_hi[:, bass.ts(a, TH)], attn_bank[not is_first(a)][:, :]).then_inc(hT_hi_ready, 1)

            def silu_unit(g, k, c):
                u = C * (NE * g + k) + c
                b = (C * k + c) % UBUF
                act.wait_ge(gate_in_ps, u + 1)
                if not isinstance(u, int) or u >= UBUF:
                    act.wait_ge(hid_ready, u - UBUF + 1)
                act.activation(silu[:, b, :], gate_ps[c][:, :], ACT.Silu,
                               scale=1.0 / (ACT_SCALE * W_SCALE)).then_inc(silu_ready, 1)

            def hid_high(g, k, c):
                s = NE * g + k
                u = C * s + c
                act.wait_ge(hid_ready, u + 1)
                act.wait_ge(y_in_ps, 1 + NE * g + max(k - NBUF + 1, 0))
                act.copy(hid_hi[:, k % NBUF, c, :], hid[:, (C * k + c) % HBUF, :]).then_inc(hid_hi_ready, 1)

            evac_qT(0, 0)
            evac_cT(0, 0)
            evac_qT(1, 1)
            evac_cT(1, 1)
            act.wait_ge(small_in, 16 * N_SMALL)
            act.activation(g_tanh[:, :], g_raw[:, :], ACT.Tanh).then_inc(tanh_ready, 1)
            act.mul(gw_hi[:, :], gw_f32[:, :], W_SCALE).then_inc(gw_hi_ready, 1)
            softmax_exp(0)
            evac_query(0)
            evac_ctxW(0)
            with act.Fori(0, N_PAIRS) as pair:
                for i in range(2):
                    a = 2 * pair + 1 + i
                    evac_qT(a + 1, i)
                    evac_cT(a + 1, i)
                    softmax_exp(a)
                    evac_query(a)
                    evac_ctxW(a)
            attn_div(0)
            evac_qT(6, 0)
            evac_cT(6, 0)
            evac_attnT(0)
            softmax_exp(5)
            evac_query(5)
            evac_ctxW(5)
            evac_qT(7, 1)
            evac_cT(7, 1)
            softmax_exp(6)
            evac_query(6)
            evac_ctxW(6)
            squares_x1(0)
            act.wait_ge(w_in[3], 48)
            weight_high(6)
            softmax_exp(7)
            norm_x1(0, 0)
            norm_x1(0, 1)
            evac_query(7)
            evac_ctxW(7)
            hT_high(0)
            weight_high(7)
            weight_high(8)
            act.wait_ge(rec_ready, 2)
            silu_unit(0, 0, 0)
            silu_unit(0, 0, 1)
            hid_high(0, 0, 0)
            silu_unit(0, 1, 0)
            hid_high(0, 0, 1)
            silu_unit(0, 1, 1)
            hid_high(0, 1, 0)

            def body(g, last=False):
                for k in range(LAG, NE if last else NE + LAG):
                    if not last and k == 8:
                        hT_high(g + 1)
                    if not last and k == 2:
                        attn_div(g + 1)
                    silu_unit(g, k, 0)
                    hid_high(g, k - 1, 1)
                    if not last and k == 7:
                        norm_x1(g + 1, 1)
                    silu_unit(g, k, 1)
                    hid_high(g, k, 0)
                    if not last:
                        if k == 5:
                            squares_x1(g + 1)
                        if k == 6:
                            norm_x1(g + 1, 0)
                        if k == 2:
                            evac_attnT(g + 1)
                if last:
                    hid_high(g, NE - 1, 1)

            with act.Fori(0, G - 1) as g:
                body(g)
            body(G - 1, last=True)

        @block.vector
        def _(dve):
            chain = {"base": 0, "n": 0}

            def link(ins):
                chain["n"] += 1
                ins.then_inc(dve_step, 1)
                dve.wait_ge(dve_step, chain["base"] + chain["n"])

            def norm_stats(src, n, mean, var):
                for t in range(n):
                    ins = dve.bn_stats(stats[:, t, :], src(t))
                link(ins)
                m_even, m_odd = stats[:, 0:n, 1], stats[:, 0:n, 4]
                m2, diff, sq = mean2[:, 0:n], half_diff[:, 0:n], sq_sum[:, 0:n]
                dve.tensor_tensor(m2, m_even, m_odd, ALU.add)
                dve.tensor_tensor(diff, m_even, m_odd, ALU.subtract)
                link(dve.tensor_tensor(sq, stats[:, 0:n, 2], stats[:, 0:n, 5], ALU.add))
                dve.tensor_scalar(mean, m2, 0.5, None, ALU.mult)
                link(dve.tensor_tensor(diff, diff, diff, ALU.mult))
                link(dve.scalar_tensor_tensor(out=sq, in0=diff, scalar=H / 4, in1=sq,
                                              op0=ALU.mult, op1=ALU.add))
                dve.tensor_scalar(var, sq, 1.0 / H, LN_EPS, ALU.mult, ALU.add).then_inc(var_ready, 1)

            def x_tile(a):
                return lambda t: x_all[:, bass.ds(a * TH + t * H, H)]

            def row_max(a):
                dve.wait_ge(score_in_ps, a + 1)
                if not is_first(a):
                    dve.wait_ge(exp_ready, a)
                dve.tensor_reduce(neg_max[:, :], score_ps[:, 0:TV].rearrange("p (t v) -> p t v", v=V),
                                  AX.X, ALU.max, negate=True).then_inc(max_ready, 1)

            def proj_tile(t):
                return proj[:, tile_cols(t)]

            def x1_tile(t):
                return x1[:, tile_cols(t)]

            def whole_proj(a):
                dve.wait_ge(proj_in_ps, a + 1)
                link(dve.tensor_tensor(proj[:, :], proj_bank[not is_first(a)][:, :], query_W[:, bass.ts(a, TH)], ALU.add))

            def stats_proj():
                norm_stats(proj_tile, T, mean[:, :], var_eps[:, :])

            def gain_proj(a):
                for t in range(T):
                    ins = dve.scalar_tensor_tensor(out=proj_tile(t), in0=proj_tile(t), scalar=mean[:, t:t + 1],
                                                   in1=gain[:, tile_cols(t)], op0=ALU.subtract, op1=ALU.mult)
                link(ins)

            def residual(a):
                dve.wait_ge(rstd_ready, norm_count(a))
                dve.wait_ge(xs_ready, a + 1)
                if not is_first(a):
                    dve.wait_ge(hn_ready, 2 * a)
                for t in range(T):
                    ins = dve.scalar_tensor_tensor(out=x1_tile(t), in0=proj_tile(t), scalar=rstd[:, t:t + 1],
                                                   in1=xs[:, tile_cols(t)], op0=ALU.mult, op1=ALU.add,
                                                   accum_out=sum_h[:, t:t + 1])
                ins.then_inc(x1_ready, 1)
                dve.wait_ge(x1_ready, a + 1)
                dve.tensor_scalar(neg_mean_sq[:, :], sum_h[:, :], -SQUARE_SCALE / H, None, ALU.mult)
                dve.tensor_scalar(neg_mean_h[:, :], sum_h[:, :], -1.0 / H, None, ALU.mult).then_inc(neg_mean_h_ready, 1)

            def hT_low(a):
                dve.wait_ge(hT_hi_ready, a + 1)
                cols = bass.ts(a, TH)
                dve.tensor_tensor(hT_lo[:, cols], attn_bank[not is_first(a)][:, :], hT_hi[:, cols],
                                  ALU.subtract).then_inc(hT_lo_ready, 1)

            def over(v):
                return v[:, :].unsqueeze(2).to_broadcast([P, T, E])

            def route_pick_first(a):
                dve.wait_ge(logit_in_ps, a + 1)
                dve.tensor_scalar(logit[:, :, :],
                                  proj_bank[not is_first(a)][:, 0:T * E].rearrange("p (t e) -> p t e", e=E),
                                  1.0 / (ACT_SCALE * W_SCALE), None, ALU.mult).then_inc(logit_read, 1)
                dve.wait_ge(logit_read, a + 1)
                link(dve.tensor_reduce(top[:, :], logit[:, :, :], AX.X, ALU.max))
                dve.tensor_tensor(below_top[:, :, :], logit[:, :, :], over(top),
                                  ALU.subtract).then_inc(below_ready, 1)
                link(dve.tensor_tensor(code[:, :, :], logit[:, :, :], over(top), ALU.is_ge))
                link(dve.tensor_tensor(code[:, :, :], code[:, :, :], first_code[:, :, :], ALU.mult))
                link(dve.tensor_reduce(best[:, :], code[:, :, :], AX.X, ALU.max))
                link(dve.tensor_tensor(one1[:, :, :], first_code[:, :, :], over(best), ALU.is_equal))

            def route_pick_second():
                link(dve.scalar_tensor_tensor(out=logit2[:, :, :], in0=one1[:, :, :], scalar=-1e30,
                                              in1=logit[:, :, :], op0=ALU.mult, op1=ALU.add))
                link(dve.tensor_reduce(top[:, :], logit2[:, :, :], AX.X, ALU.max))
                link(dve.tensor_tensor(code[:, :, :], logit2[:, :, :], over(top), ALU.is_ge))
                link(dve.tensor_tensor(code[:, :, :], code[:, :, :], first_code[:, :, :], ALU.mult))
                link(dve.tensor_reduce(best[:, :], code[:, :, :], AX.X, ALU.max))
                link(dve.tensor_tensor(one2[:, :, :], first_code[:, :, :], over(best), ALU.is_equal))
                link(dve.tensor_tensor(picked[:, :, :], one1[:, :, :], one2[:, :, :], ALU.add))

            def route_weights(a):
                dve.wait_ge(expo_ready, T * (a + 1))
                dve.tensor_reduce(sum_all[:, :], expo[:, :, :], AX.X, ALU.add)
                link(dve.tensor_tensor(chosen[:, :, :], expo[:, :, :], picked[:, :, :], ALU.mult))
                link(dve.tensor_reduce(sum_two[:, :], chosen[:, :, :], AX.X, ALU.add))
                link(dve.scalar_tensor_tensor(out=sum_two[:, :], in0=sum_all[:, :], scalar=TOPK_EPS,
                                              in1=sum_two[:, :], op0=ALU.mult, op1=ALU.add))
                link(dve.reciprocal(sum_two[:, :], sum_two[:, :]))
                link(dve.tensor_scalar(sum_two[:, :], sum_two[:, :], ffn_gain[:, 0:1], None, ALU.mult))
                link(dve.tensor_tensor(weight[:, :, :], chosen[:, :, :], over(sum_two), ALU.mult))

            def hid_unit(g, k, c):
                u = C * (NE * g + k) + c
                b = (C * k + c) % UBUF
                dve.wait_ge(up_in_ps, u + 1)
                dve.wait_ge(silu_ready, u + 1)
                if not isinstance(u, int) or u >= HBUF:
                    dve.wait_ge(y_in_ps, 1 + NE * g + k - HBUF // C + 1)
                dve.scalar_tensor_tensor(out=hid[:, (C * k + c) % HBUF, :], in0=up_ps[c][:, :],
                                         scalar=HID_SCALE / (ACT_SCALE * W_SCALE), in1=silu[:, b, :],
                                         op0=ALU.mult, op1=ALU.mult).then_inc(hid_ready, 1)

            def add_y(g, k):
                s = NE * g + k
                dve.wait_ge(y_in_ps, 1 + s + 1)
                dve.wait_ge(y_added, 1 + s)
                if k == 0:
                    ins = dve.scalar_tensor_tensor(out=x_all[:, bass.ts(g, TH)], in0=y_ps[0][:, :],
                                                   scalar=ffn_gain[:, 0:1], in1=x1[:, :], op0=ALU.mult, op1=ALU.add)
                else:
                    for t in range(T):
                        xt = x_tile(g)(t)
                        ins = dve.scalar_tensor_tensor(out=xt, in0=y_ps[k % 2][:, tile_cols(t)],
                                                       scalar=weight[:, t, k - 1:k], in1=xt,
                                                       op0=ALU.mult, op1=ALU.add)
                ins.then_inc(y_added, 1)

            def norm_x(a, buf):
                dve.wait_ge(rstd_ready, a + 1)
                if not (isinstance(a, int) and a < 2):
                    dve.wait_ge(xT_in_ps, a - 1)
                for t in range(T):
                    ins = dve.tensor_scalar(xn[:, buf, tile_cols(t)], x_tile(a)(t), mean_x[:, buf, t:t + 1],
                                            rstd_x[:, buf, t:t + 1], ALU.subtract, ALU.mult)
                ins.then_inc(xn_ready, 1)

            def stats_x(a, buf):
                norm_stats(x_tile(a), T, mean_x[:, buf, :], var_x[:, buf, :])

            def attn_reciprocals(lo, hi):
                dve.wait_ge(exp_ready, hi)
                cols = slice(lo * T, hi * T)
                dve.reciprocal(attn_rec[:, cols], expd_sum[:, cols]).then_inc(rec_ready, 1)

            def weight_low(e):
                dve.wait_ge(w_hi_pool, e + 1)
                dve.scalar_tensor_tensor(out=w_lo[:, e, :, :], in0=w_f32[:, e, :, :], scalar=W_SCALE,
                                         in1=w_hi[:, e, :, :], op0=ALU.mult, op1=ALU.subtract).then_inc(w_lo_dve, 1)

            dve.wait_ge(x_in[0], 16)
            stats_x(0, 0)
            dve.wait_ge(x_in[1], 16)
            stats_x(1, 1)
            norm_x(0, 0)
            dve.wait_ge(y_in_ps, 1)
            dve.tensor_copy(w_ctx_T[:, :], w_T_ps[:, 0:H])
            dve.tensor_copy(w_qry_T[:, :], w_T_ps[:, H:2 * H]).then_inc(y_added, 1)
            norm_x(1, 1)
            dve.wait_ge(x_in[2], 16)
            stats_x(2, 0)
            stats_x(3, 1)
            norm_x(2, 0)
            row_max(0)
            attn_reciprocals(0, 1)
            dve.wait_ge(x_in[3], 16)
            before = chain["n"]
            per_pair = 8
            with dve.Fori(0, N_PAIRS) as pair:
                chain["base"], chain["n"] = before + pair * per_pair, 0
                for i in range(2):
                    a = 2 * pair + 1 + i
                    stats_x(a + 3, i)
                    row_max(a)
                    norm_x(a + 2, (1 + i) % 2)
                assert chain["n"] == per_pair, chain["n"]
            chain["base"], chain["n"] = 0, before + N_PAIRS * per_pair
            norm_x(7, 1)
            dve.wait_ge(tanh_ready, 1)
            dve.tensor_scalar(gain[:, :], gain[:, :], g_tanh[:, 0:1], None, ALU.mult).then_inc(gain_ready, 1)
            dve.tensor_scalar(shift[:, :], shift[:, :], g_tanh[:, 0:1], None, ALU.mult).then_inc(gain_ready, 1)
            link(dve.tensor_scalar(ffn_gain[:, :], g_tanh[:, 1:2], 1.0 / (HID_SCALE * W_SCALE), None, ALU.mult))
            row_max(5)
            weight_low(0)
            whole_proj(0)
            stats_proj()
            row_max(6)
            gain_proj(0)
            residual(0)
            row_max(7)
            for e in range(1, DVE_LOW):
                weight_low(e)
            hT_low(0)
            attn_reciprocals(1, G)
            dve.wait_ge(gw_hi_ready, 1)
            dve.scalar_tensor_tensor(out=gw_lo[:, :], in0=gw_f32[:, :], scalar=W_SCALE, in1=gw_hi[:, :],
                                     op0=ALU.mult, op1=ALU.subtract).then_inc(gw_ready, 1)
            route_pick_first(0)
            route_pick_second()
            for k in range(LAG):
                for c in range(C):
                    hid_unit(0, k, c)

            def body(g, last=False):
                for k in range(LAG, NE + LAG):
                    if k < NE or not last:
                        hid_unit(g, k, 0)
                    if k == 3:
                        route_weights(g)
                    if not last:
                        if k == 4:
                            stats_proj()
                        if k == 5:
                            residual(g + 1)
                        if k == 8:
                            hT_low(g + 1)
                        if k == 9:
                            route_pick_first(g + 1)
                        if k == 10:
                            route_pick_second()
                    if k < NE or not last:
                        hid_unit(g, k, 1)
                    if not last:
                        if k == 3:
                            whole_proj(g + 1)
                        if k == 4:
                            gain_proj(g + 1)
                    add_y(g, k - LAG)

            before = chain["n"]
            per_body = 24
            with dve.Fori(0, G - 1) as g:
                chain["base"], chain["n"] = before + g * per_body, 0
                body(g)
                assert chain["n"] == per_body, chain["n"]
            chain["base"], chain["n"] = before + (G - 1) * per_body, 0
            body(G - 1, last=True)

        @block.tensor
        def _(pe):
            def transpose_in(a, buf, landed):
                pe.wait_ge(xn_ready, a + 1)
                if not is_first(a):
                    pe.wait_ge(qT_ready, a)
                for t in range(T):
                    ins = pe.transpose(bank_a[:, tile_cols(t)], xn[:, buf, tile_cols(t)], ident[:, :])
                ins.then_inc(xT_in_ps, 1)
                pe.wait_ge(ctx_landed[buf], 16 * landed)
                if not is_first(a):
                    pe.wait_ge(cT_ready, a)
                for t in range(T):
                    ins = pe.transpose(bank_b[:, tile_cols(t, V)], ctx_in[:, buf, t, :], ident[0:V, 0:V])
                ins.then_inc(ctxT_in_ps, 1)

            def scores(a, buf):
                pe.wait_ge(qT_ready, a + 1)
                pe.wait_ge(cT_ready, a + 1)
                if not is_first(a):
                    pe.wait_ge(exp_ready, a)
                for t in range(T):
                    ins = pe.matmul(score_ps[:, tile_cols(t, V)], qT[:, buf, tile_cols(t)],
                                    cT[:, buf, tile_cols(t, V)], start=True, stop=True)
                ins.then_inc(score_in_ps, 1)
                if not is_first(a):
                    pe.wait_ge(query_ready, a)
                for t in range(T):
                    ins = pe.matmul(query_ps[:, tile_cols(t)], qT[:, buf, tile_cols(t)], w_qry_T[:, :],
                                    start=True, stop=True)
                ins.then_inc(query_in_ps, 1)
                if not is_first(a):
                    pe.wait_ge(ctxW_ready, a)
                for t in range(T):
                    ins = pe.matmul(ctxW_ps[0:V, tile_cols(t)], cT[:, buf, tile_cols(t, V)], w_ctx_T[:, :],
                                    start=True, stop=True)
                ins.then_inc(ctxW_in_ps, 1)

            def transpose_attn(a):
                pe.wait_ge(attn_ready, a + 1)
                if not is_first(a):
                    pe.wait_ge(hT_lo_ready, a)
                for t in range(T):
                    ins = pe.transpose(attn_bank[not is_first(a)][0:V, tile_cols(t)], attn[:, t, :], ident[:, :])
                ins.then_inc(attnT_in_ps, 1)

            def project(a):
                pe.wait_ge(attnT_ready, a + 1)
                if is_first(a):
                    pe.wait_ge(small_in, 16 * N_SMALL)
                else:
                    pe.wait_ge(logit_read, a)
                for t in range(T):
                    ins = pe.matmul(proj_bank[not is_first(a)][:, tile_cols(t)], attnT[:, tile_cols(t)],
                                    ctxW[:, bass.ds(a * TH + t * H, H)], start=True, stop=True)
                ins.then_inc(proj_in_ps, 1)

            def transpose_h(a):
                pe.wait_ge(hn_ready, 2 * (a + 1))
                for t in range(T):
                    ins = pe.transpose(attn_bank[not is_first(a)][:, tile_cols(t)], hn[:, tile_cols(t)], ident[:, :])
                ins.then_inc(hT_in_ps, 1)

            def route_logits(a):
                pe.wait_ge(hT_lo_ready, a + 1)
                for t in range(T):
                    cols = bass.ds(a * TH + t * S, S)
                    o = proj_bank[not is_first(a)][:, tile_cols(t, E)]
                    pe.matmul(o, hT_hi[:, cols], gw_hi[:, :], start=True, stop=False)
                    pe.matmul(o, hT_hi[:, cols], gw_lo[:, :], start=False, stop=False)
                    ins = pe.matmul(o, hT_lo[:, cols], gw_hi[:, :], start=False, stop=True)
                ins.then_inc(logit_in_ps, 1)

            def gate_up(g, k, c):
                s = NE * g + k
                u = C * s + c
                cols = bass.ts(g + k // NE, TH)
                for part, bank, free, done in ((0, gate_ps[c], silu_ready, gate_in_ps),
                                               (1, up_ps[c], hid_ready, up_in_ps)):
                    wh, wl = parts(part, k % NE)
                    if not isinstance(u, int) or u >= C:
                        pe.wait_ge(free, u - 1)
                    pe.matmul(bank[:, :], wh[:, c:D:C], hT_hi[:, cols], start=True, stop=False)
                    pe.matmul(bank[:, :], wh[:, c:D:C], hT_lo[:, cols], start=False, stop=False)
                    pe.matmul(bank[:, :], wl[:, c:D:C], hT_hi[:, cols], start=False,
                              stop=True).then_inc(done, 1)

            def down(g, k):
                s = NE * g + k
                wh, wl = parts(2, k)
                o = y_ps[k % 2]
                pe.wait_ge(hid_lo_ready, C * (s + 1))
                pe.wait_ge(y_added, 1 + (s if k == 0 else s - 1))
                for t in range(T):
                    for c in range(C):
                        hh = hid_hi[:, k % NBUF, c, tile_cols(t)]
                        hl = hid_lo[:, k % NBUF, c, tile_cols(t)]
                        pe.matmul(o[:, tile_cols(t)], hh, wh[:, tile_cols(c, P)], start=(c == 0), stop=False)
                        pe.matmul(o[:, tile_cols(t)], hh, wl[:, tile_cols(c, P)], start=False, stop=False)
                        ins = pe.matmul(o[:, tile_cols(t)], hl, wh[:, tile_cols(c, P)], start=False,
                                        stop=(c == C - 1))
                ins.then_inc(y_in_ps, 1)

            pe.wait_ge(ident_ready, 1)
            pe.wait_ge(w_rows_in, 16)
            pe.transpose(w_T_ps[:, 0:H], w_rows[:, 0:H], ident[:, :])
            pe.transpose(w_T_ps[:, H:2 * H], w_rows[:, H:2 * H], ident[:, :]).then_inc(y_in_ps, 1)
            transpose_in(0, 0, 1)
            transpose_in(1, 1, 1)
            pe.wait_ge(y_added, 1)
            scores(0, 0)
            with pe.Fori(0, N_PAIRS) as pair:
                for i in range(2):
                    a = 2 * pair + 1 + i
                    transpose_in(a + 1, i, pair + 2)
                    scores(a, (1 + i) % 2)
            transpose_in(6, 0, 4)
            transpose_attn(0)
            scores(5, 1)
            project(0)
            transpose_in(7, 1, 4)
            scores(6, 0)
            scores(7, 1)
            transpose_h(0)
            pe.wait_ge(exp_ready, G)
            pe.wait_ge(query_ready, G)
            pe.wait_ge(ctxW_ready, G)
            pe.wait_ge(gw_ready, 1)
            route_logits(0)
            pe.wait_ge(logit_read, 1)
            for k in range(LAG):
                pe.wait_ge(w_lo_dve, k + 1)
                for c in range(C):
                    gate_up(0, k, c)

            def body(g, last=False):
                for k in range(LAG, NE + LAG):
                    if k < DVE_LOW:
                        pe.wait_ge(w_lo_dve, k + 1)
                    elif k < NE:
                        pe.wait_ge(w_lo_pool, k - DVE_LOW + 1)
                    if not last and k == 9:
                        route_logits(g + 1)
                    if k < NE or not last:
                        gate_up(g, k, 0)
                    if not last and k == 3:
                        project(g + 1)
                    if k < NE or not last:
                        gate_up(g, k, 1)
                    if not last and k == 2:
                        transpose_attn(g + 1)
                    down(g, k - LAG)
                    if not last and k == 7:
                        transpose_h(g + 1)

            with pe.Fori(0, G - 1) as g:
                body(g)
            body(G - 1, last=True)


_INS = ["x", "ctx_1024", "g_xattn", "g_ffn", "L0_xattn_W", "L0_xattn_b", "L0_xattn_gamma", "L0_xattn_beta",
        "L0_ffn_gate_w", "L0_ffn_w_gate", "L0_ffn_w_up", "L0_ffn_w_down", "L0_ffn_ws_gate", "L0_ffn_ws_up",
        "L0_ffn_ws_down"]


def kernel(**inputs):
    import numpy as _np
    import concourse.bacc as _bacc
    from concourse import mybir as _mybir
    from concourse.bass_utils import run_bass_kernel_spmd as _run

    nc = _bacc.Bacc("TRN2", target_bir_lowering=False, num_devices=1)
    arrays, args = {}, []
    for name in _INS:
        a = _np.ascontiguousarray(inputs[name])
        arrays[f"in_{name}"] = a
        args.append(nc.dram_tensor(f"in_{name}", a.shape, _mybir.dt.from_np(a.dtype), kind="ExternalInput").ap())
    shape = inputs["x"].shape
    args.append(nc.dram_tensor("out_0", shape, _mybir.dt.float32, kind="ExternalOutput").ap())
    flamingo_gated_layer(nc, *args)
    r = _run(nc, [arrays], core_ids=[0])
    return r.results[0]["out_0"]
```
